# Optimizing a Trainium2 kernel written in Bass

```python
import numpy as np
import jax
import jax.numpy as jnp

def _softmax(x, axis=-1):
    return jax.nn.softmax(x, axis=axis)

def _gelu(x):
    return jax.nn.gelu(x, approximate=True)

def _silu(x):
    return jax.nn.silu(x)

def _sigmoid(x):
    return jax.nn.sigmoid(x)

def _layernorm(x, axis=-1, eps=1e-05):
    m = jnp.mean(x, axis=axis, keepdims=True)
    v = jnp.var(x, axis=axis, keepdims=True)
    return (x - m) / jnp.sqrt(v + eps)

def _scatter_add(tgt, idx, src, axis=0):
    return tgt.at[idx].add(src)

def _segment_sum(src, seg, n):
    return jax.ops.segment_sum(src, seg, n)
kernel_name = 'mk_adaln_attn_ffn_d1_seqx_r4_7d7228'

def setup_inputs(seed: int=0):
    np.random.seed(seed)
    _w = jnp.asarray

    def _rec_inputs():
        import jax
        import jax.numpy as jnp
        _rk = jax.random.key(seed)
        x = -0.000125 + 0.9999 * jax.random.normal(jax.random.fold_in(_rk, 1), (4, 512, 256), jnp.float32)
        _lenS = 512 - jax.random.randint(jax.random.fold_in(_rk, 7), (4,), 0, max(1, 512 // 4) + 1, jnp.int32)
        _lenS2 = 512 - jax.random.randint(jax.random.fold_in(_rk, 8), (4,), 0, max(1, 512 // 4) + 1, jnp.int32)
        cond_512 = 0.0061147 + 1.02565 * jax.random.normal(jax.random.fold_in(_rk, 11), (4, 128), jnp.float32)
        return (x, cond_512)
    x, cond_512 = _rec_inputs()

    def _L0_cond_setup():
        import jax, jax.numpy as jnp
        import numpy as np
        B, S, D, H, C = (8, 1024, 256, 64, 128)
        INIT_RANGE = 0.01
        key = jax.random.key(seed)
        ks = jax.random.split(key, 6)
        return {'hidden_states': jax.random.normal(ks[0], (B, S, D), dtype=jnp.float32), 'conditions': jax.random.normal(ks[1], (B, C), dtype=jnp.float32), 'down_project': jax.random.normal(ks[2], (D, H), dtype=jnp.float32) * INIT_RANGE, 'down_gamma': jax.random.normal(ks[3], (C, H), dtype=jnp.float32), 'down_beta': jnp.zeros((C, H), dtype=jnp.float32), 'up_project': jax.random.normal(ks[4], (H, D), dtype=jnp.float32) * INIT_RANGE, 'up_gamma': jax.random.normal(ks[5], (C, D), dtype=jnp.float32), 'up_beta': jnp.zeros((C, D), dtype=jnp.float32)}
    _L0_cond_all = _L0_cond_setup()
    _L0_cond_in = {k: v for k, v in _L0_cond_all.items() if k in ('down_project', 'down_gamma', 'down_beta', 'up_project', 'up_gamma', 'up_beta')}
    del _L0_cond_all

    def _L0_attn_setup():
        import jax, jax.numpy as jnp
        import numpy as np
        B, T, D_MODEL = (2, 256, 256)
        H, DEPTH = (8, 5)
        DH = D_MODEL // H
        key = jax.random.key(seed)
        k_x, k_wp, k_bp, k_wv, k_wo = jax.random.split(key, 5)
        x = jax.random.normal(k_x, (B, T, D_MODEL), dtype=jnp.float32)
        Wp = jax.random.normal(k_wp, (D_MODEL, H * DEPTH), dtype=jnp.float32) * 0.02
        bp = jnp.zeros((H * DEPTH,), dtype=jnp.float32)
        Wv = jax.random.normal(k_wv, (D_MODEL, D_MODEL), dtype=jnp.float32) * 0.02
        Wo = jax.random.normal(k_wo, (D_MODEL, D_MODEL), dtype=jnp.float32) * 0.02
        return {'x': x, 'Wp': Wp, 'bp': bp, 'Wv': Wv, 'Wo': Wo}
    _L0_attn_all = _L0_attn_setup()
    _L0_attn_in = {k: v for k, v in _L0_attn_all.items() if k in ('Wp', 'bp', 'Wv', 'Wo')}
    del _L0_attn_all

    def _L0_cond2_setup():
        import jax, jax.numpy as jnp
        import numpy as np
        IN_DIM = 256
        OUT_DIM = 256
        MU_DIM = 128
        K = 30
        key = jax.random.key(seed)
        k1, k2, k3, k4, k5 = jax.random.split(key, 5)
        B, S = (16, 512)
        x = jax.random.normal(k1, (B, S, IN_DIM), dtype=jnp.float32)
        mu = jax.random.normal(k2, (B, MU_DIM), dtype=jnp.float32)
        W_dec = jax.random.normal(k3, (MU_DIM, (IN_DIM + 1) * K), dtype=jnp.float32) / np.sqrt(MU_DIM)
        b_dec = jax.random.normal(k4, ((IN_DIM + 1) * K,), dtype=jnp.float32) * 0.01
        V = jax.random.normal(k5, (K, OUT_DIM), dtype=jnp.float32) / np.sqrt(K)
        return {'x': x, 'mu': mu, 'W_dec': W_dec, 'b_dec': b_dec, 'V': V}
    _L0_cond2_all = _L0_cond2_setup()
    _L0_cond2_in = {k: v for k, v in _L0_cond2_all.items() if k in ('W_dec', 'b_dec', 'V')}
    del _L0_cond2_all

    def _L0_ffn_setup():
        import jax, jax.numpy as jnp
        import numpy as np
        B, S, H, E = (2, 2048, 256, 8)
        SCALE = 0.5
        key = jax.random.key(seed)
        k1, k2 = jax.random.split(key)
        x = jax.random.normal(k1, (B, S, H), dtype=jnp.float32)
        gate_w = jax.random.normal(k2, (E, H), dtype=jnp.float32) * 0.02
        coeff = SCALE * (1.0 + 0.05 * jnp.arange(E, dtype=jnp.float32))
        expert_w = coeff[:, None, None] * jnp.eye(H, dtype=jnp.float32)
        return {'x': x, 'gate_w': gate_w, 'expert_w': expert_w}
    _L0_ffn_all = _L0_ffn_setup()
    _L0_ffn_in = {k: v for k, v in _L0_ffn_all.items() if k in ('gate_w', 'expert_w')}
    del _L0_ffn_all
    return {'x': x, 'cond_512': cond_512, 'L0_cond_down_project': _L0_cond_in['down_project'], 'L0_cond_down_gamma': _L0_cond_in['down_gamma'], 'L0_cond_down_beta': _L0_cond_in['down_beta'], 'L0_cond_up_project': _L0_cond_in['up_project'], 'L0_cond_up_gamma': _L0_cond_in['up_gamma'], 'L0_cond_up_beta': _L0_cond_in['up_beta'], 'L0_attn_Wp': _L0_attn_in['Wp'], 'L0_attn_bp': _L0_attn_in['bp'], 'L0_attn_Wv': _L0_attn_in['Wv'], 'L0_attn_Wo': _L0_attn_in['Wo'], 'L0_cond2_W_dec': _L0_cond2_in['W_dec'], 'L0_cond2_b_dec': _L0_cond2_in['b_dec'], 'L0_cond2_V': _L0_cond2_in['V'], 'L0_ffn_gate_w': _L0_ffn_in['gate_w'], 'L0_ffn_expert_w': _L0_ffn_in['expert_w']}

def reference(x, cond_512, L0_cond_down_project, L0_cond_down_gamma, L0_cond_down_beta, L0_cond_up_project, L0_cond_up_gamma, L0_cond_up_beta, L0_attn_Wp, L0_attn_bp, L0_attn_Wv, L0_attn_Wo, L0_cond2_W_dec, L0_cond2_b_dec, L0_cond2_V, L0_ffn_gate_w, L0_ffn_expert_w):
    import jax
    import jax.numpy as jnp

    def _L0_cond_ref(hidden_states, conditions, down_project, down_gamma, down_beta, up_project, up_gamma, up_beta):
        import jax, jax.numpy as jnp
        import numpy as np
        B, S, D, H, C = (8, 1024, 256, 64, 128)
        INIT_RANGE = 0.01
        dg = conditions @ down_gamma
        db = conditions @ down_beta
        ug = conditions @ up_gamma
        ub = conditions @ up_beta
        w_down = down_project[None, :, :] * dg[:, None, :] + db[:, None, :]
        down = jnp.einsum('bsd,bdh->bsh', hidden_states, w_down)
        act = jax.nn.relu(down)
        w_up = up_project[None, :, :] * ug[:, None, :] + ub[:, None, :]
        up = jnp.einsum('bsh,bhd->bsd', act, w_up)
        return up + hidden_states

    def _L0_attn_ref(x, Wp, bp, Wv, Wo):
        import jax, jax.numpy as jnp
        import numpy as np
        B, T, D_MODEL = (2, 256, 256)
        H, DEPTH = (8, 5)
        DH = D_MODEL // H
        Bx, Tx, d = x.shape
        paths = jax.nn.sigmoid(x @ Wp + bp)
        paths = paths.reshape(Bx, Tx, H, DEPTH).transpose(0, 2, 1, 3)
        pq = paths[:, :, :, None, :]
        pk = paths[:, :, None, :, :]
        agree = pq * pk + (1.0 - pq) * (1.0 - pk)
        sim = jnp.cumprod(agree, axis=-1).sum(axis=-1) / DEPTH
        mask = jnp.triu(jnp.ones((Tx, Tx), dtype=bool), k=1)
        sim = jnp.where(mask[None, None], -jnp.inf, sim)
        attn = jax.nn.softmax(sim, axis=-1)
        V = (x @ Wv).reshape(Bx, Tx, H, DH).transpose(0, 2, 1, 3)
        ctx = jnp.einsum('bhqk,bhkd->bhqd', attn, V)
        ctx = ctx.transpose(0, 2, 1, 3).reshape(Bx, Tx, d)
        return ctx @ Wo

    def _L0_cond2_ref(x, mu, W_dec, b_dec, V):
        import jax, jax.numpy as jnp
        import numpy as np
        IN_DIM = 256
        OUT_DIM = 256
        MU_DIM = 128
        K = 30
        B = mu.shape[0]
        U = (mu @ W_dec + b_dec).reshape(B, IN_DIM + 1, K)
        param = jnp.einsum('bik,kj->bij', U, V)
        weight = param[:, :-1, :]
        bias = param[:, -1, :]
        out = jnp.einsum('bsd,bde->bse', x, weight)
        out = out + bias[:, None, :]
        return out

    def _L0_ffn_ref(x, gate_w, expert_w):
        import jax, jax.numpy as jnp
        import numpy as np
        B, S, H, E = (2, 2048, 256, 8)
        SCALE = 0.5
        scores = jnp.einsum('bsh,eh->bse', x, gate_w)
        chosen = jnp.argmax(scores, axis=-1)
        onehot = jax.nn.one_hot(chosen, gate_w.shape[0], dtype=x.dtype)
        expert_out = jnp.einsum('bsh,efh->bsef', x, expert_w)
        return x + jnp.einsum('bsef,bse->bsf', expert_out, onehot)
    x = x + _L0_attn_ref(_L0_cond_ref(x, cond_512, L0_cond_down_project, L0_cond_down_gamma, L0_cond_down_beta, L0_cond_up_project, L0_cond_up_gamma, L0_cond_up_beta), L0_attn_Wp, L0_attn_bp, L0_attn_Wv, L0_attn_Wo)
    x = x + _L0_ffn_ref(_L0_cond2_ref(x, cond_512, L0_cond2_W_dec, L0_cond2_b_dec, L0_cond2_V), L0_ffn_gate_w, L0_ffn_expert_w)
    return x

_drawn_inputs = setup_inputs


def setup_inputs(seed=0):
    import zlib

    import numpy as np

    out = dict(_drawn_inputs(seed))
    spreads = {'L0_cond_down_beta': (0.0, 0.1), 'L0_cond_up_beta': (0.0, 0.1), 'L0_attn_bp': (0.0, 0.8)}
    factors = {'L0_cond_down_project': 8.0,
     'L0_cond_down_gamma': 8.0,
     'L0_cond_up_project': 3.507,
     'L0_cond_up_gamma': 3.316,
     'L0_attn_Wp': 4.167,
     'L0_cond2_b_dec': 5.494,
     'L0_ffn_gate_w': 3.769}
    for name, (base, spread) in spreads.items():
        noise = np.random.default_rng([zlib.crc32(name.encode()), seed]).standard_normal(out[name].shape)
        drawn = base * np.exp(spread * noise) if base else spread * noise
        out[name] = jnp.asarray(drawn.astype(out[name].dtype))
    for name, factor in factors.items():
        out[name] = (out[name] * factor).astype(out[name].dtype)
    return out
```

```python
from contextlib import ExitStack

import concourse.bass as bass
from concourse import mybir

F32 = mybir.dt.float32
F16 = mybir.dt.float16
ALU = mybir.AluOpType
ACT = mybir.ActivationFunctionType
AX_X = mybir.AxisListType.X

P = 128
B, T, D = 4, 512, 256
TT = T // P
DC = D // P
HD = 64
H, DEPTH = 8, 5
DH = D // H
NF = 2 ** DEPTH
HG = 4
NG = H // HG
K = 30
KP = 32
E = 8
CW = 2 * P
U_COLS = D * K // 4
U_PIECE = U_COLS // 4

UNITS = [(0, 0, 256, True, False), (1, 128, 128, True, True),
         (0, 256, 256, False, False), (1, 256, 256, False, False), (2, 256, 256, True, False),
         (3, 384, 128, True, True)]
NU = len(UNITS)
BU = NG * NU
ALL = B * BU


def unit(u):
    return u // BU, u % BU // NU, UNITS[u % NU]


def diagonals(u):
    return sum(unit(i)[2][3] for i in range(u + 1))


def chunks(u):
    return sum(unit(i)[2][4] for i in range(u + 1))


PROLOGUE = [("cond",), ("gdn",), ("xT", 0, 0), ("gup", 0), ("xT", 0, 1), ("down", 0), ("gup", 1), ("up", 0, 0),
            ("up", 0, 1), ("gup", 2),
            ("VL", 0, 0), ("VL", 0, 1), ("VL", 0, 2), ("VL", 0, 3), ("gup", 3), ("xT", 1, 0), ("xT", 1, 1), ("wT",),
            ("phi", 0, 0), ("phi", 0, 1), ("woT",), ("down", 1), ("Q",), ("up", 1, 0), ("up", 1, 1), ("start",)]


def between(b):
    nxt, prv = b + 1, b - 1
    gaps = [[] for _ in range(BU)]
    if b == 0:
        gaps[0] += [("VL", 1, 0), ("VL", 1, 1)]
        gaps[1] += [("VL", 1, 2), ("VL", 1, 3)]
        gaps[2] += [("U", 0), ("U", 1)]
        gaps[3] += [("U", 2), ("U", 3)]
        gaps[4] += [("phi", 1, 0), ("phi", 1, 1)]
        gaps[5] += [("ubT",), ("eT", 0), ("eT", 1)]
        gaps[6] += [("eT", 2), ("eT", 3)]
        gaps[7] += [("Uadd",), ("G", 0), ("eT", 4), ("eT", 5)]
        gaps[8] += [("eT", 6), ("eT", 7)]
        gaps[9] += [("WoU",), ("G", 1)]
        gaps[10] += [("xT", 2, 0), ("xT", 2, 1)]
        return gaps
    if nxt < B:
        gaps[0] += [("down", nxt)]
        gaps[1] += [("up", nxt, 0), ("up", nxt, 1)]
        gaps[2] += [("VL", nxt, 0)]
        gaps[3] += [("VL", nxt, 1)]
        gaps[4] += [("VL", nxt, 2)]
        gaps[5] += [("VL", nxt, 3)]
        gaps[7] += [("phi", nxt, 0), ("phi", nxt, 1)]
        if nxt + 1 < B:
            gaps[10] += [("xT", nxt + 1, 0), ("xT", nxt + 1, 1)]
    gaps[1] += [("zT", prv)]
    gaps[2] += [("zs", prv)]
    gaps[6] += [("zoT", prv, 0), ("zoT", prv, 1)]
    gaps[8] += [("out", prv, 0)]
    gaps[9] += [("out", prv, 1)]
    return gaps


ORDER = list(PROLOGUE)
for _b in range(B):
    for _i, _gap in enumerate(between(_b)):
        ORDER += [("unit", _b * BU + _i)] + _gap
ORDER += [("zT", B - 1), ("zs", B - 1), ("zoT", B - 1, 0), ("zoT", B - 1, 1), ("out", B - 1, 0), ("out", B - 1, 1)]
WORK = {s: n for n, s in enumerate(s for s in ORDER if s[0] not in ("unit", "start", "Uadd"))}


def build(nc, x, cond, down_project, down_gamma, down_beta, up_project, up_gamma, up_beta, Wp, bp, Wv, Wo,
          W_dec, b_dec, V, gate_w, expert_w, out):
    with ExitStack() as ctx:
        def sb(name, shape, dt=F32):
            return ctx.enter_context(nc.sbuf_tensor(name, shape, dt))

        def ps(name, shape, dt=F32):
            return ctx.enter_context(nc.psum_tensor(name, shape, dt))

        def sem(name):
            return ctx.enter_context(nc.semaphore(name))

        x_nat = sb("x_nat", [P, B, TT, D])
        cond_nat = sb("cond_nat", [B, P])
        gam_dn = sb("gam_dn", [P, 2 * HD])
        gam_up = sb("gam_up", [P, 2 * D])
        dproj = sb("dproj", [P, DC, HD])
        uproj = sb("uproj", [P, D])
        w_vl = sb("w_vl", [P, DC, D + H * DEPTH])
        bp_b = sb("bp_b", [P, H * DEPTH])
        wo = sb("wo", [P, DC, D])
        wdec = sb("wdec", [P, (D + 1) * K])
        bdec = sb("bdec", [P, DC, K])
        bdec_row = sb("bdec_row", [B, K])
        v4 = sb("v4", [P, D])
        gate = sb("gate", [E, D])
        ex_nat = sb("ex_nat", [P, E, DC, D])
        ident = sb("ident", [P, P])
        level = sb("level", [P, HG, NF])
        level_d = sb("level_d", [P, HG * NF])
        rootc = sb("rootc", [P, 1])
        ones = sb("ones", [P, DH])
        rank8 = sb("rank8", [P, TT, E])
        cond_b = sb("cond_b", [P, B, P])
        cond_c = sb("cond_c", [P, KP])
        w_tmp = sb("w_tmp", [P, B * DC * HD])
        u_tmp = sb("u_tmp", [P, D])
        w_dn = sb("w_dn", [P, B, DC, HD])
        w_up = sb("w_up", [P, B, D])
        u_row = sb("u_row", [P, U_COLS + K])
        u_raw = sb("u_raw", [P, DC, B, K])
        u_w = sb("u_w", [P, DC, B, KP])
        ub_row = sb("ub_row", [B, TT, KP])
        ub_col = sb("ub_col", [P, B])
        wt = sb("wt", [P, DC * P + DC * E])
        wo_t = sb("wo_t", [P, DC, D])
        wo_u = sb("wo_u", [P, DC, B * KP])
        q_bd = sb("q_bd", [P, TT, E])
        ex_t = wdec[:, 0:E * DC * D].rearrange("p (e c f) -> p e c f", e=E, c=DC)
        gexp = sb("gexp", [P, 2, D])
        x_t = sb("x_t", [P, 3, DC, T])
        act_t = sb("act_t", [P, T // 2])
        h_t = sb("h_t", [P, DC, T])
        v_sb = sb("v_sb", [P, 2, TT, D])
        logit = sb("logit", [P, TT, H * DEPTH])
        sign = sb("sign", [P, TT * H, DEPTH])
        feat = sb("feat", [P, TT * H, NF])
        feat_h = sb("feat_h", [P, NG, 5 * T], F16)
        st = sb("st", [P, 2, NG, HG, 2 * T], F16)
        prob = sb("prob", [P, 3, HG, CW])
        rden = sb("rden", [P, CW])
        ctx_t = sb("ctx_t", [P, 2, NG, T])
        z_t = sb("z_t", [P, P])
        z_nat = sb("z_nat", [P, TT, KP])
        smax = sb("smax", [P, TT])
        kmax = sb("kmax", [P, TT])
        hit = sb("hit", [P, TT, E])
        key = sb("key", [P, TT, E])
        pick = sb("pick", [P, TT, E])
        zo = sb("zo", [P, TT, E, KP])
        zo_t = sb("zo_t", [P, 2, T])
        u_dram = nc.dram_tensor("u_scratch", (B, D * K), F32, kind="Internal").ap()
        s_ps = ps("s_ps", [P, 2, HG, CW])
        c_ps = [ps(f"c_ps{i}", [P, 2 * CW]) for i in range(2)]
        work = [ps(f"work{i}", [P, T]) for i in range(2)]

        ld_cond, ld_gdn, ld_gup, ld_dp, ld_up, ld_vl, ld_bp = [sem("ld_" + n) for n in
                                                             ("cond", "gdn", "gup", "dp", "up", "vl", "bp")]
        ld_wo, ld_wdec, ld_bdec, ld_v, ld_gate, ld_ex = [sem("ld_" + n) for n in
                                                         ("wo", "wdec", "bdec", "v", "gate", "ex")]
        ld_x = [sem(f"ld_x{b}") for b in range(B)]
        v_zero = sem("v_zero")
        ident_ready = sem("ident_ready")
        consts = sem("consts")
        rootc_ready = sem("rootc_ready")
        cond_ready = sem("cond_ready")
        wdn_ready = sem("wdn_ready")
        wup_ready = sem("wup_ready")
        filled = sem("filled")
        emptied = [sem(f"emptied{i}") for i in range(2)]
        logit_ready = sem("logit_ready")
        sign_ready = sem("sign_ready")
        feat_ready = sem("feat_ready")
        stacked = [sem(f"stacked{b}") for b in range(B)]
        halves_ready = sem("halves_ready")
        scored = sem("scored")
        exped = sem("exped")
        masked = sem("masked")
        summed = sem("summed")
        ctx_ready = sem("ctx_ready")
        u_rows = sem("u_rows")
        u_stored = sem("u_stored")
        u_moved = sem("u_moved")
        u_ready = sem("u_ready")
        zo_ready = sem("zo_ready")
        chain_v = sem("chain_v")
        chain_p = sem("chain_p")
        stored = sem("stored")

        def full(eng, step):
            eng.wait_ge(filled, WORK[step] + 1)

        def done(eng, step):
            eng.wait_ge(emptied[WORK[step] % 2], WORK[step] // 2 + 1)

        def bank(step):
            return work[WORK[step] % 2]

        def empty(step):
            return emptied[WORK[step] % 2]

        block = ctx.enter_context(nc.Block())

        @block.sync
        def _(sp):
            sp.dma_start(cond_nat[:], cond).then_inc(ld_cond, 16)
            sp.dma_start(gam_dn[:, 0:HD], down_gamma).then_inc(ld_gdn, 16)
            sp.dma_start(gam_dn[:, HD:2 * HD], down_beta).then_inc(ld_gdn, 16)
            sp.dma_start(x_nat[:, 0], x[0].rearrange("(t p) d -> p t d", p=P)).then_inc(ld_x[0], 16)
            sp.dma_start(w_vl[:, :, 0:D], Wv.rearrange("(c p) n -> p c n", p=P)).then_inc(ld_vl, 16)
            sp.dma_start(w_vl[:, :, D:], Wp.rearrange("(c p) n -> p c n", p=P)).then_inc(ld_vl, 16)
            for b in range(1, B):
                sp.dma_start(x_nat[:, b], x[b].rearrange("(t p) d -> p t d", p=P)).then_inc(ld_x[b], 16)
                if b == 1:
                    sp.dma_start(wdec[:], W_dec).then_inc(ld_wdec, 16)
                    sp.dma_start(ex_nat[:], expert_w.rearrange("e (c p) h -> p e c h", p=P)).then_inc(ld_ex, 16)
            for s in ORDER:
                if s[0] == "phi" and s[2] == NG - 1:
                    b = s[1]
                    sp.wait_ge(halves_ready, NG * (b + 1))
                    if b >= 2:
                        sp.wait_ge(scored, BU * (b - 1))
                    for q, pair in enumerate((0, 1, 3, 2)):
                        for h in range(HG):
                            sp.dma_start(st[NF * q:NF * (q + 1), b % 2, :, h, :],
                                         feat_h[NF * h:NF * (h + 1), :, T * pair:T * (pair + 2)]
                                         ).then_inc(stacked[b], 16)
                elif s == ("U", 3):
                    done(sp, s)
                    for j in range(4):
                        sp.dma_start(u_dram[:, U_COLS * j:U_COLS * (j + 1)], u_row[KP * j:KP * j + B, 0:U_COLS]
                                     ).then_inc(u_stored, 16)
                    sp.wait_ge(u_stored, 16 * 4)
                    for c in range(DC):
                        sp.dma_start(u_raw[:, c], u_dram[:, P * K * c:P * K * (c + 1)].rearrange(
                            "b (p k) -> p b k", k=K)).then_inc(u_moved, 16)
                elif s[0] == "out":
                    _, b, h = s
                    done(sp, s)
                    sp.dma_start(out[b, 2 * P * h:2 * P * (h + 1), :].rearrange("(t p) d -> p t d", p=P),
                                 x_nat[:, b, 2 * h:2 * h + 2, :]).then_inc(stored, 16)
            sp.wait_ge(stored, 16 * 2 * B)

        @block.gpsimd
        def _(pool):
            nc.gpsimd.memset(ident[:], 0.0).then_inc(chain_p, 1)
            pool.wait_ge(chain_p, 1)
            nc.gpsimd.affine_select(out=ident[:], in_=ident[:], compare_op=ALU.not_equal, fill=1.0, base=0,
                                    pattern=[[-1, P]], channel_multiplier=1).then_inc(ident_ready, 1)
            nc.gpsimd.memset(v4[:], 0.0).then_inc(v_zero, 1)
            pool.dma_start(bp_b[:], bp.rearrange("(a n) -> a n", a=1).broadcast_to([P, H * DEPTH])
                           ).then_inc(ld_bp, 16)
            pool.wait_ge(v_zero, 1)
            for j in range(4):
                pool.dma_start(v4[KP * j:KP * j + K, :], V).then_inc(ld_v, 16)
            pool.dma_start(gate[:], gate_w).then_inc(ld_gate, 16)
            pool.dma_start(bdec[:], b_dec[0:D * K].rearrange("(c p k) -> p c k", p=P, k=K)).then_inc(ld_bdec, 16)
            pool.dma_start(bdec_row[:], b_dec[D * K:].rearrange("(a k) -> a k", a=1).broadcast_to([B, K])
                           ).then_inc(ld_bdec, 16)
            for m in range(DEPTH + 1):
                lo, hi = (0, 1) if m == 0 else (2 ** (m - 1), 2 ** m)
                c = (2.0 ** (1 - max(m, 1)) - 2.0 ** -DEPTH) / DEPTH
                nc.gpsimd.memset(level[:, :, lo:hi], c ** 0.5)
            for e in range(E):
                nc.gpsimd.memset(rank8[:, :, e:e + 1], float(E - e))
            nc.gpsimd.memset(feat[:, :, 0:1], 1.0)
            nc.gpsimd.memset(ones[:], 1.0)
            nc.gpsimd.memset(q_bd[:], 0.0)
            nc.gpsimd.memset(u_w[:], 0.0)
            nc.gpsimd.memset(ub_row[:], 0.0).then_inc(consts, 1)
            links = 1
            for s in ORDER:
                if s == ("start",) or s[0] == "unit":
                    for u in (0, 1) if s == ("start",) else (s[1] + 2,):
                        if u < ALL and unit(u)[2][3]:
                            pool.wait_ge(exped, u + 1)
                            tri = prob[:, u % 3, :, 0:P]
                            nc.gpsimd.affine_select(out=tri, in_=tri, compare_op=ALU.is_ge, fill=0.0, base=0,
                                                    pattern=[[0, HG], [1, P]], channel_multiplier=-1
                                                    ).then_inc(masked, 1)
                elif s[0] == "VL" and s[2] == TT - 1:
                    b = s[1]
                    pool.wait_ge(sign_ready, b + 1)
                    if b >= 1:
                        full(pool, ("phi", b - 1, NG - 1))
                    nc.gpsimd.tensor_copy(feat[:, :, 1:2], sign[:, :, 0:1]).then_inc(chain_p, 1)
                    for i in range(1, DEPTH):
                        n = 2 ** i
                        links += 1
                        pool.wait_ge(chain_p, links)
                        nc.gpsimd.tensor_tensor(feat[:, :, n:2 * n], feat[:, :, 0:n],
                                                sign[:, :, i:i + 1].broadcast_to([P, TT * H, n]), ALU.mult
                                                ).then_inc(feat_ready if i == DEPTH - 1 else chain_p, 1)
                elif s[0] == "zs":
                    b = s[1]
                    done(pool, s)
                    for t in range(TT):
                        ins = nc.gpsimd.tensor_tensor(zo[:, t], z_nat[:, t:t + 1, :].broadcast_to([P, E, KP]),
                                                      pick[:, t, :].unsqueeze(2).broadcast_to([P, E, KP]), ALU.mult)
                    ins.then_inc(zo_ready, 1)

        @block.scalar
        def _(act):
            act.dma_start(gam_up[:, 0:D], up_gamma).then_inc(ld_gup, 16)
            act.dma_start(gam_up[:, D:2 * D], up_beta).then_inc(ld_gup, 16)
            act.dma_start(dproj[:], down_project.rearrange("(c p) n -> p c n", p=P)).then_inc(ld_dp, 16)
            act.dma_start(uproj[0:HD, :], up_project).then_inc(ld_up, 16)
            act.dma_start(uproj[HD:2 * HD, :], up_project).then_inc(ld_up, 16)
            act.dma_start(wo[:], Wo.rearrange("(c p) n -> p c n", p=P)).then_inc(ld_wo, 16)
            for s in ORDER:
                if s == ("start",) or s[0] == "unit":
                    for u in (0, 1) if s == ("start",) else (s[1] + 2,):
                        if u < ALL:
                            n = unit(u)[2][2]
                            act.wait_ge(scored, u + 1)
                            if u >= 3:
                                act.wait_ge(summed, u - 2)
                            nc.scalar.activation(prob[:, u % 3, :, 0:n], s_ps[:, u % 2, :, 0:n],
                                                 ACT.Exp).then_inc(exped, 1)
                elif s[0] == "xT":
                    full(act, s)
                    nc.scalar.copy(x_t[:, s[1] % 3, s[2], :], bank(s)[:]).then_inc(empty(s), 1)
                elif s[0] == "VL":
                    _, b, t = s
                    full(act, s)
                    act.wait_ge(logit_ready, TT * b + t + 1)
                    nc.scalar.copy(v_sb[:, b % 2, t, :], bank(s)[:, 0:D]).then_inc(empty(s), 1)
                    if t == TT - 1:
                        if b >= 1:
                            act.wait_ge(feat_ready, b)
                        nc.scalar.activation(sign[:], logit[:].rearrange("p t (h l) -> p (t h) l", l=DEPTH),
                                             ACT.Tanh, scale=0.5).then_inc(sign_ready, 1)
                elif s[0] == "wT":
                    full(act, s)
                    nc.scalar.copy(wt[:], bank(s)[:, 0:DC * (P + E)]).then_inc(empty(s), 1)
                elif s[0] == "woT":
                    full(act, s)
                    nc.scalar.copy(wo_t[:].rearrange("p c n -> p (c n)"), bank(s)[:]).then_inc(empty(s), 1)
                elif s[0] == "eT":
                    full(act, s)
                    nc.scalar.copy(ex_t[:, s[1]].rearrange("p c n -> p (c n)"), bank(s)[:]).then_inc(empty(s), 1)
                elif s[0] == "zoT":
                    full(act, s)
                    nc.scalar.copy(zo_t[:, s[2], :], bank(s)[:]).then_inc(empty(s), 1)

        @block.vector
        def _(dve):
            links = [0]

            def link(ins):
                links[0] += 1
                ins.then_inc(chain_v, 1)
                dve.wait_ge(chain_v, links[0])

            dve.wait_ge(consts, 1)
            dve.wait_ge(ident_ready, 1)
            link(nc.vector.tensor_tensor(level_d[:], level[:].rearrange("p h f -> p (h f)"), ident[:], ALU.mult))
            nc.vector.reduce_sum(rootc[:], level_d[:], AX_X).then_inc(rootc_ready, 1)
            nc.vector.memset(cond_c[:], 0.0)
            for s in ORDER:
                kind = s[0]
                if kind == "cond":
                    full(dve, s)
                    link(nc.vector.tensor_copy(cond_b[:], bank(s)[:, 0:B].unsqueeze(2).broadcast_to([P, B, P])))
                    nc.vector.tensor_copy(cond_c[:, 0:B], bank(s)[:, 0:B]).then_inc(empty(s), 1)
                elif kind == "gdn":
                    g = bank(s)[:].rearrange("p (b n) -> p b n", b=B)
                    dve.wait_ge(ld_dp, 16)
                    full(dve, s)
                    for b in range(B):
                        w3 = w_tmp[:].rearrange("p (b c n) -> p b c n", b=B, c=DC)
                        ins = nc.vector.tensor_tensor(w3[:, b], dproj[:],
                                                      g[:, b:b + 1, 0:HD].broadcast_to([P, DC, HD]), ALU.mult)
                    link(ins)
                    for b in range(B):
                        ins = nc.vector.tensor_tensor(w_dn[:, b], w3[:, b],
                                                      g[:, b:b + 1, HD:2 * HD].broadcast_to([P, DC, HD]), ALU.add)
                    ins.then_inc(empty(s), 1)
                elif kind == "gup":
                    b = s[1]
                    dve.wait_ge(ld_up, 32)
                    full(dve, s)
                    link(nc.vector.tensor_tensor(u_tmp[:], uproj[:], bank(s)[:, 0:D], ALU.mult))
                    nc.vector.tensor_tensor(w_up[:, b, :], u_tmp[:], bank(s)[:, D:2 * D], ALU.add
                                            ).then_inc(empty(s), 1)
                elif kind == "down":
                    full(dve, s)
                    nc.vector.tensor_scalar(act_t[:], bank(s)[:, 0:T // 2], 0.0, None, ALU.max
                                            ).then_inc(empty(s), 1)
                elif kind == "up":
                    _, b, j = s
                    full(dve, s)
                    half = slice(T // 2 * j, T // 2 * (j + 1))
                    nc.vector.tensor_tensor(h_t[:, :, half], bank(s)[:].rearrange("p (c t) -> p c t", c=DC),
                                            x_t[:, b % 3, :, half], ALU.add).then_inc(empty(s), 1)
                elif kind == "VL":
                    _, b, t = s
                    if t == 0:
                        dve.wait_ge(ld_bp, 16)
                        if b >= 1:
                            dve.wait_ge(sign_ready, b)
                    full(dve, s)
                    nc.vector.tensor_tensor(logit[:, t, :], bank(s)[:, D:D + H * DEPTH], bp_b[:], ALU.add
                                            ).then_inc(logit_ready, 1)
                elif kind == "phi":
                    _, b, g = s
                    dve.wait_ge(rootc_ready, 1)
                    full(dve, s)
                    if b >= 1:
                        dve.wait_ge(stacked[b - 1], 16 * 4 * HG)
                    slots = feat_h[:, g, :].rearrange("p (n t) -> p n t", t=T)
                    link(nc.vector.tensor_scalar(slots[:, 0, :], bank(s)[:], rootc[:], None, ALU.mult))
                    nc.vector.scalar_tensor_tensor(out=slots[:, 2, :], in0=bank(s)[:], scalar=rootc[:],
                                                   in1=slots[:, 0, :], op0=ALU.mult, op1=ALU.subtract
                                                   ).then_inc(empty(s), 1)
                    nc.vector.tensor_copy(slots[:, 1, :], slots[:, 0, :])
                    nc.vector.tensor_copy(slots[:, 4, :], slots[:, 0, :])
                    done(dve, s)
                    nc.vector.tensor_copy(slots[:, 3, :], slots[:, 2, :]).then_inc(halves_ready, 1)
                elif kind == "Q":
                    full(dve, s)
                    for j in range(TT):
                        ins = nc.vector.tensor_copy(q_bd[KP * j:KP * j + KP, j, :], bank(s)[KP * j:KP * j + KP, 0:E])
                    ins.then_inc(empty(s), 1)
                elif kind == "U":
                    m = s[1]
                    if m == 3:
                        dve.wait_ge(ld_bdec, 32)
                        full(dve, s)
                        nc.vector.tensor_tensor(ub_row[:, :, 0:K],
                                                bank(s)[0:B, U_PIECE:U_PIECE + K].unsqueeze(1).broadcast_to([B, TT, K]),
                                                bdec_row[:].unsqueeze(1).broadcast_to([B, TT, K]), ALU.add)
                    full(dve, s)
                    nc.vector.tensor_copy(u_row[:, U_PIECE * m:U_PIECE * (m + 1)], bank(s)[:, 0:U_PIECE]
                                          ).then_inc(empty(s), 1)
                elif kind == "ubT":
                    full(dve, s)
                    nc.vector.tensor_copy(ub_col[:], bank(s)[:, 0:B]).then_inc(empty(s), 1)
                elif kind == "Uadd":
                    dve.wait_ge(u_moved, 16 * DC)
                    for c in range(DC):
                        ins = nc.vector.tensor_tensor(u_w[:, c, :, 0:K], u_raw[:, c],
                                                      bdec[:, c:c + 1, :].broadcast_to([P, B, K]), ALU.add)
                    ins.then_inc(u_ready, 1)
                elif kind == "WoU":
                    full(dve, s)
                    nc.vector.tensor_copy(wo_u[:].rearrange("p c n -> p (c n)"), bank(s)[:, 0:DC * P]
                                          ).then_inc(empty(s), 1)
                elif kind == "G":
                    full(dve, s)
                    nc.vector.tensor_tensor(gexp[:, s[1], :], bank(s)[:, 0:D], v4[:], ALU.add
                                            ).then_inc(empty(s), 1)
                elif kind == "unit":
                    u = s[1]
                    b, g, (_, _, _, _, last) = unit(u)
                    if last:
                        n = chunks(u) - 1
                        lo = CW * (n % 2)
                        dve.wait_ge(summed, u + 1)
                        if n >= 1:
                            dve.wait_ge(ctx_ready, n)
                        link(nc.vector.reciprocal(rden[:], c_ps[n % 2][:, CW:2 * CW]))
                        nc.vector.tensor_tensor(ctx_t[:, b % 2, g, lo:lo + CW], c_ps[n % 2][:, 0:CW], rden[:],
                                                ALU.mult).then_inc(ctx_ready, 1)
                elif kind == "zT":
                    full(dve, s)
                    nc.vector.tensor_scalar(z_t[:], bank(s)[:, 0:P], ub_col[:, s[1]:s[1] + 1], None, ALU.add
                                            ).then_inc(empty(s), 1)
                elif kind == "zs":
                    b = s[1]
                    sc = bank(s)[:, P:P + TT * E].rearrange("p (t e) -> p t e", e=E)
                    full(dve, s)
                    if b >= 1:
                        dve.wait_ge(zo_ready, b)
                    nc.vector.tensor_copy(z_nat[:].rearrange("p t k -> p (t k)"), bank(s)[:, 0:P])
                    link(nc.vector.reduce_max(smax[:], sc, AX_X))
                    link(nc.vector.tensor_tensor(hit[:], sc, smax[:].unsqueeze(2).broadcast_to([P, TT, E]),
                                                 ALU.is_ge))
                    link(nc.vector.tensor_tensor(key[:], hit[:], rank8[:], ALU.mult))
                    link(nc.vector.reduce_max(kmax[:], key[:], AX_X))
                    nc.vector.tensor_tensor(pick[:], key[:], kmax[:].unsqueeze(2).broadcast_to([P, TT, E]),
                                            ALU.is_equal).then_inc(empty(s), 1)
                elif kind == "out":
                    _, b, h = s
                    full(dve, s)
                    xs = x_nat[:, b, 2 * h:2 * h + 2, :]
                    nc.vector.tensor_tensor(xs, bank(s)[:].rearrange("p (t d) -> p t d", t=2), xs, ALU.add
                                            ).then_inc(empty(s), 1)

        @block.tensor
        def _(pe):
            def mm(o, w, r, start=True, stop=True):
                return nc.tensor.matmul(o, w, r, start=start, stop=stop, skip_group_check=True)

            def scores(u):
                b, g, (kt, q0, n, _, _) = unit(u)
                if u % BU == 0:
                    pe.wait_ge(stacked[b], 16 * 4 * HG)
                if u >= 2:
                    pe.wait_ge(exped, u - 1)
                for h in range(HG):
                    ins = mm(s_ps[:, u % 2, h, 0:n],
                             st[:, b % 2, g, h, P * kt:P * (kt + 1)], st[:, b % 2, g, h, T + q0:T + q0 + n])
                ins.then_inc(scored, 1)

            def context(u):
                b, g, (kt, q0, n, diagonal, last) = unit(u)
                if diagonal:
                    pe.wait_ge(masked, diagonals(u))
                pe.wait_ge(exped, u + 1)
                m = chunks(u) - last
                if kt == 0:
                    if m >= 2:
                        pe.wait_ge(ctx_ready, m - 1)
                    if u % BU == 0:
                        done(pe, ("VL", b, TT - 1))
                lo = q0 % CW
                for h in range(HG):
                    mm(c_ps[m % 2][DH * h:DH * (h + 1), lo:lo + n],
                       v_sb[:, b % 2, kt, DH * (HG * g + h):DH * (HG * g + h + 1)], prob[:, u % 3, h, 0:n],
                       start=(kt == 0), stop=last)
                for h in range(HG):
                    ins = mm(c_ps[m % 2][DH * h:DH * (h + 1), CW + lo:CW + lo + n], ones[:], prob[:, u % 3, h, 0:n],
                             start=False, stop=last)
                ins.then_inc(summed, 1)

            pe.wait_ge(ident_ready, 1)
            for s in ORDER:
                kind = s[0]
                if kind == "start":
                    pe.wait_ge(consts, 1)
                    scores(0)
                    scores(1)
                    continue
                if kind == "unit":
                    context(s[1])
                    if s[1] + 2 < ALL:
                        scores(s[1] + 2)
                    continue
                if kind == "Uadd":
                    continue
                n = WORK[s]
                o = bank(s)
                if n >= 2:
                    pe.wait_ge(emptied[n % 2], n // 2)
                if kind == "cond":
                    pe.wait_ge(ld_cond, 16)
                    ins = nc.tensor.transpose(o[:, 0:B], cond_nat[:], ident[0:B, 0:B])
                elif kind == "gdn":
                    done(pe, ("cond",))
                    pe.wait_ge(ld_gdn, 32)
                    for b in range(B):
                        ins = mm(o[:, P * b:P * (b + 1)], cond_b[:, b, :], gam_dn[:])
                elif kind == "gup":
                    if s[1] == 0:
                        pe.wait_ge(ld_gup, 32)
                    ins = mm(o[:], cond_b[:, s[1], :], gam_up[:])
                elif kind == "xT":
                    _, b, c = s
                    if c == 0:
                        pe.wait_ge(ld_x[b], 16)
                    for t in range(TT):
                        ins = nc.tensor.transpose(o[:, P * t:P * (t + 1)], x_nat[:, b, t, P * c:P * (c + 1)], ident[:])
                elif kind == "down":
                    b = s[1]
                    if b == 0:
                        done(pe, ("gdn",))
                    for c in range(DC):
                        done(pe, ("xT", b, c))
                    for c in range(DC):
                        for j in range(2):
                            ins = mm(o[HD * j:HD * (j + 1), 0:T // 2], w_dn[:, b, c, :],
                                     x_t[:, b % 3, c, T // 2 * j:T // 2 * (j + 1)], start=(c == 0), stop=(c == DC - 1))
                elif kind == "up":
                    _, b, j = s
                    if j == 0:
                        done(pe, ("gup", b))
                        done(pe, ("down", b))
                    for c in range(DC):
                        ins = mm(o[:, T // 2 * c:T // 2 * (c + 1)], w_up[HD * j:HD * (j + 1), b, P * c:P * (c + 1)],
                                 act_t[HD * j:HD * (j + 1), :])
                elif kind == "VL":
                    _, b, t = s
                    if t == 0:
                        if b == 0:
                            pe.wait_ge(ld_vl, 32)
                        done(pe, ("up", b, 0))
                        done(pe, ("up", b, 1))
                    for c in range(DC):
                        ins = mm(o[:, 0:D + H * DEPTH], h_t[:, c, P * t:P * (t + 1)], w_vl[:, c, :],
                                 start=(c == 0), stop=(c == DC - 1))
                elif kind == "phi":
                    _, b, g = s
                    pe.wait_ge(feat_ready, b + 1)
                    for t in range(TT):
                        ins = nc.tensor.transpose(
                            o[:, P * t:P * (t + 1)],
                            feat[:, H * t + HG * g:H * t + HG * (g + 1), :].rearrange("p h f -> p (h f)"), ident[:])
                elif kind == "wT":
                    pe.wait_ge(ld_v, 16 * 4)
                    pe.wait_ge(ld_gate, 16)
                    for c in range(DC):
                        nc.tensor.transpose(o[:, P * c:P * (c + 1)], v4[:, P * c:P * (c + 1)], ident[:])
                        ins = nc.tensor.transpose(o[:, DC * P + E * c:DC * P + E * (c + 1)],
                                                  gate[:, P * c:P * (c + 1)], ident[0:E, 0:E])
                elif kind == "woT":
                    pe.wait_ge(ld_wo, 16)
                    for d in range(DC):
                        for c in range(DC):
                            ins = nc.tensor.transpose(o[:, D * d + P * c:D * d + P * (c + 1)],
                                                      wo[:, c, P * d:P * (d + 1)], ident[:])
                elif kind == "Q":
                    done(pe, ("wT",))
                    for c in range(DC):
                        ins = mm(o[:, 0:E], wt[:, P * c:P * (c + 1)], wt[:, DC * P + E * c:DC * P + E * (c + 1)],
                                 start=(c == 0), stop=(c == DC - 1))
                elif kind == "U":
                    m = s[1]
                    if m == 0:
                        pe.wait_ge(ld_wdec, 16)
                    for j in range(4):
                        lo = U_COLS * j + U_PIECE * m
                        ins = mm(o[KP * j:KP * (j + 1), 0:U_PIECE], cond_c[:], wdec[:, lo:lo + U_PIECE])
                    if m == 3:
                        ins = mm(o[0:KP, U_PIECE:U_PIECE + K], cond_c[:], wdec[:, D * K:(D + 1) * K])
                elif kind == "ubT":
                    done(pe, ("U", 3))
                    ins = nc.tensor.transpose(o[:, 0:B], ub_row[:].rearrange("b j k -> b (j k)"), ident[0:B, 0:B])
                elif kind == "WoU":
                    pe.wait_ge(u_ready, 1)
                    done(pe, ("woT",))
                    for c in range(DC):
                        for d in range(DC):
                            ins = mm(o[:, P * c:P * (c + 1)], wo_t[:, d, P * c:P * (c + 1)],
                                     u_w[:, d].rearrange("p b k -> p (b k)"), start=(d == 0), stop=(d == DC - 1))
                elif kind == "eT":
                    e = s[1]
                    if e == 0:
                        pe.wait_ge(ld_ex, 16)
                    for hc in range(DC):
                        for fc in range(DC):
                            ins = nc.tensor.transpose(o[:, D * hc + P * fc:D * hc + P * (fc + 1)],
                                                      ex_nat[:, e, fc, P * hc:P * (hc + 1)], ident[:])
                elif kind == "G":
                    for e in range(4):
                        done(pe, ("eT", 4 * s[1] + e))
                    for hc in range(DC):
                        for j in range(4):
                            ins = mm(o[KP * j:KP * (j + 1), 0:D], wt[:, P * hc:P * hc + KP],
                                     ex_t[:, 4 * s[1] + j, hc, :], start=(hc == 0), stop=(hc == DC - 1))
                elif kind == "zT":
                    b = s[1]
                    if b == 0:
                        done(pe, ("ubT",))
                        done(pe, ("WoU",))
                    pe.wait_ge(ctx_ready, 2 * NG * (b + 1))
                    for c in range(2 * DC):
                        for t in range(TT):
                            w = u_w[:, c, b, :] if c < DC else wo_u[:, c - DC, KP * b:KP * (b + 1)]
                            r = x_t[:, b % 3, c, P * t:P * (t + 1)] if c < DC else ctx_t[:, b % 2, c - DC, P * t:P * (t + 1)]
                            ins = mm(o[KP * t:KP * (t + 1), 0:P], w, r, start=(c == 0), stop=(c == 2 * DC - 1))
                elif kind == "zs":
                    done(pe, ("zT", s[1]))
                    if s[1] == 0:
                        done(pe, ("Q",))
                    nc.tensor.transpose(o[:, 0:P], z_t[:], ident[:])
                    ins = mm(o[:, P:P + TT * E], z_t[:], q_bd[:].rearrange("p t e -> p (t e)"))
                elif kind == "zoT":
                    _, b, hf = s
                    pe.wait_ge(zo_ready, b + 1)
                    for t in range(TT):
                        ins = nc.tensor.transpose(o[:, P * t:P * (t + 1)],
                                                  zo[:, t, 4 * hf:4 * hf + 4, :].rearrange("p e k -> p (e k)"), ident[:])
                elif kind == "out":
                    _, b, hf = s
                    if hf == 0:
                        if b == 0:
                            done(pe, ("G", 0))
                            done(pe, ("G", 1))
                        done(pe, ("zoT", b, 0))
                        done(pe, ("zoT", b, 1))
                    for i in range(2):
                        t = 2 * hf + i
                        tok = slice(P * t, P * (t + 1))
                        for c in range(2 * DC):
                            w = ctx_t[:, b % 2, c, tok] if c < DC else zo_t[:, c - DC, tok]
                            r = wo[:, c, :] if c < DC else gexp[:, c - DC, :]
                            ins = mm(o[:, D * i:D * (i + 1)], w, r, start=(c == 0), stop=(c == 2 * DC - 1))
                ins.then_inc(filled, 1)


NAMES = ["x", "cond_512", "L0_cond_down_project", "L0_cond_down_gamma", "L0_cond_down_beta", "L0_cond_up_project",
         "L0_cond_up_gamma", "L0_cond_up_beta", "L0_attn_Wp", "L0_attn_bp", "L0_attn_Wv", "L0_attn_Wo",
         "L0_cond2_W_dec", "L0_cond2_b_dec", "L0_cond2_V", "L0_ffn_gate_w", "L0_ffn_expert_w"]


def kernel(**inputs):
    import numpy as np
    import concourse.bacc as bacc
    from concourse.bass_utils import run_bass_kernel_spmd as run

    nc = bacc.Bacc("TRN2", target_bir_lowering=False, num_devices=1)
    arrays, args = {}, []
    for name in NAMES:
        a = np.ascontiguousarray(inputs[name])
        arrays["in_" + name] = a
        args.append(nc.dram_tensor("in_" + name, a.shape, mybir.dt.from_np(a.dtype), kind="ExternalInput").ap())
    args.append(nc.dram_tensor("out_x", (B, T, D), F32, kind="ExternalOutput").ap())
    build(nc, *args)
    return run(nc, [arrays], core_ids=[0]).results[0]["out_x"]
```

```python
from contextlib import ExitStack

import concourse.bass as bass
from concourse import mybir

F32 = mybir.dt.float32
F16 = mybir.dt.float16
ALU = mybir.AluOpType
ACT = mybir.ActivationFunctionType
AX_X = mybir.AxisListType.X

P = 128
B, T, D = 4, 512, 256
TT = T // P
DC = D // P
HD = 64
H, DEPTH = 8, 5
DH = D // H
NF = 2 ** DEPTH
HG = 4
NG = H // HG
K = 30
KP = 32
E = 8
CW = 2 * P
U_COLS = D * K // 4
U_PIECE = U_COLS // 4

UNITS = [(g, *u) for chunk in (((0, 0, 256, True, False), (1, 128, 128, True, True)),
                               ((0, 256, 256, False, False), (1, 256, 256, False, False), (2, 256, 256, True, False),
                                (3, 384, 128, True, True))) for g in range(NG) for u in chunk]
BU = len(UNITS)
ALL = B * BU
BC = 2 * NG
RING = 4
LONG = 4


def unit(u):
    return u // BU, UNITS[u % BU]


def diagonals(u):
    return sum(unit(i)[1][4] for i in range(u + 1))


def chunks(u):
    return sum(unit(i)[1][5] for i in range(u + 1))


def place(u):
    first = u
    while first % BU and not unit(first - 1)[1][5]:
        first -= 1
    return chunks(u) - unit(u)[1][5], u - first


def long(m):
    return m % BC >= NG


def longs(m):
    return sum(long(i) for i in range(m + 1))


def adds(u):
    return sum(long(place(i)[0]) and place(i)[1] > 0 for i in range(min(u + 1, ALL)))


ALL_T, FIRST, SECOND = (0, 1, 2, 3), (0, 1), (2, 3)
PROLOGUE = [("cond",), ("gdn",), ("gup", 0), ("xT", 0, 0), ("xT", 0, 1), ("down", 0), ("gup", 1), ("up", 0, 0),
            ("up", 0, 1), ("gup", 2), ("VL", 0, 0), ("VL", 0, 1), ("VL", 0, 2), ("VL", 0, 3), ("gup", 3), ("xT", 1, 0),
            ("xT", 1, 1), ("wT",), ("woT",), ("down", 1), ("Q",), ("up", 1, 0), ("up", 1, 1),
            ("phi", 0, 0), ("phi", 0, 1), ("U", 0), ("U", 1), ("U", 2), ("U", 3), ("VL", 1, 0), ("VL", 1, 1),
            ("VL", 1, 2), ("VL", 1, 3), ("ubT",), ("eT", 0), ("eT", 1), ("eT", 2), ("eT", 3), ("phi", 1, 0),
            ("phi", 1, 1), ("G", 0), ("eT", 4), ("eT", 5), ("eT", 6), ("eT", 7), ("Uadd",), ("start",)]


def between(b):
    n1, n2, prv = b + 1, b + 2, b - 1
    gaps = [[] for _ in range(BU)]
    if b == 0:
        gaps[0] += [("G", 1)]
        gaps[1] += [("WoU",)]
    elif n1 < B:
        gaps[0] += [("VL", n1, 0), ("VL", n1, 1)]
        gaps[1] += [("VL", n1, 2), ("VL", n1, 3)]
        gaps[4] += [("phi", n1, 0), ("phi", n1, 1)]
    if n2 < B:
        gaps[5] += [("xT", n2, 0), ("xT", n2, 1)]
        gaps[8] += [("down", n2)]
        gaps[10] += [("up", n2, 0), ("up", n2, 1)]
    if prv >= 0:
        gaps[2] += [("zT", prv, ALL_T)]
        gaps[3] += [("zs", prv, ALL_T)]
        gaps[6] += [("zoT", prv, 0), ("zoT", prv, 1)]
        gaps[7] += [("out", prv, 0)]
        gaps[9] += [("out", prv, 1)]
    if b == B - 1:
        gaps[7] += [("zT", b, FIRST)]
        gaps[8] += [("zs", b, FIRST)]
        gaps[10] += [("zoT", b, 0)]
        gaps[11] += [("out", b, 0)]
    return gaps


ORDER = list(PROLOGUE)
_open = []
for _b in range(B):
    for _i, _gap in enumerate(between(_b)):
        _u = _b * BU + _i
        ORDER += [("unit", _u)] + _open
        _m = place(_u)[0]
        _open = [("den", _m)] if UNITS[_i][5] and long(_m) else []
        ORDER += _gap
ORDER += _open + [("zT", B - 1, SECOND), ("zs", B - 1, SECOND), ("zoT", B - 1, 1), ("out", B - 1, 1)]
WORK = {s: n for n, s in enumerate(s for s in ORDER if s[0] not in ("unit", "den", "start", "Uadd"))}


def build(nc, x, cond, down_project, down_gamma, down_beta, up_project, up_gamma, up_beta, Wp, bp, Wv, Wo,
          W_dec, b_dec, V, gate_w, expert_w, out):
    with ExitStack() as ctx:
        def sb(name, shape, dt=F32):
            return ctx.enter_context(nc.sbuf_tensor(name, shape, dt))

        def ps(name, shape, dt=F32):
            return ctx.enter_context(nc.psum_tensor(name, shape, dt))

        def sem(name):
            return ctx.enter_context(nc.semaphore(name))

        x_nat = sb("x_nat", [P, B, TT, D])
        cond_nat = sb("cond_nat", [B, P])
        gam_dn = sb("gam_dn", [P, 2 * HD])
        gam_up = sb("gam_up", [P, 2 * D])
        dproj = sb("dproj", [P, DC, HD])
        uproj = sb("uproj", [P, D])
        w_vl = sb("w_vl", [P, DC, D + H * DEPTH])
        bp_b = sb("bp_b", [P, H * DEPTH])
        wo = sb("wo", [P, DC, D])
        wdec = sb("wdec", [P, (D + 1) * K])
        bdec = sb("bdec", [P, DC, K])
        bdec_row = sb("bdec_row", [B, K])
        v4 = sb("v4", [P, D])
        gate = sb("gate", [E, D])
        ex_nat = sb("ex_nat", [P, E, DC, D])
        ident = sb("ident", [P, P])
        level = sb("level", [P, HG, NF])
        level_d = sb("level_d", [P, HG * NF])
        rootc = sb("rootc", [P, 1])
        ones = sb("ones", [P, DH])
        rank8 = sb("rank8", [P, TT, E])
        cond_b = sb("cond_b", [P, B, P])
        cond_c = sb("cond_c", [P, KP])
        w_tmp = sb("w_tmp", [P, B * DC * HD])
        u_tmp = sb("u_tmp", [P, D])
        w_dn = sb("w_dn", [P, B, DC, HD])
        w_up = sb("w_up", [P, B, D])
        u_row = sb("u_row", [P, U_COLS + K])
        u_raw = sb("u_raw", [P, DC, B, K])
        u_w = sb("u_w", [P, DC, B, KP])
        ub_row = sb("ub_row", [B, TT, KP])
        ub_col = sb("ub_col", [P, B])
        wt = sb("wt", [P, DC * P + DC * E])
        wo_t = sb("wo_t", [P, DC, D])
        wo_u = sb("wo_u", [P, DC, B * KP])
        q_bd = sb("q_bd", [P, TT, E])
        ex_t = wdec[:, 0:E * DC * D].rearrange("p (e c f) -> p e c f", e=E, c=DC)
        tiles = wdec[:, E * DC * D:E * DC * D + 2 * HG * CW].rearrange("p (i h q) -> p i h q", i=2, h=HG)
        gexp = sb("gexp", [P, 2, D])
        x_t = sb("x_t", [P, 3, DC, T])
        act_t = sb("act_t", [P, T // 2])
        h_t = sb("h_t", [P, DC, T])
        v_sb = sb("v_sb", [P, 2, TT, D])
        logit = sb("logit", [P, TT, H * DEPTH])
        sign = sb("sign", [P, TT * H, DEPTH])
        feat = sb("feat", [P, TT * H, NF])
        feat_h = sb("feat_h", [P, NG, 5 * T], F16)
        st = sb("st", [P, 2, NG, HG, 2 * T], F16)
        prob = sb("prob", [P, RING, HG, CW])
        rden = sb("rden", [P, CW])
        ctx_t = sb("ctx_t", [P, 2, NG, T])
        z_t = sb("z_t", [P, P])
        z_nat = sb("z_nat", [P, TT, KP])
        smax = sb("smax", [P, TT])
        kmax = sb("kmax", [P, TT])
        hit = sb("hit", [P, TT, E])
        key = sb("key", [P, TT, E])
        pick = sb("pick", [P, TT, E])
        zo = sb("zo", [P, TT, E, KP])
        zo_t = wdec[:, E * DC * D + 2 * HG * CW:E * DC * D + 2 * HG * CW + 2 * T].rearrange("p (c t) -> p c t", c=2)
        u_dram = nc.dram_tensor("u_scratch", (B, D * K), F32, kind="Internal").ap()
        s_ps = ps("s_ps", [P, 2, HG, CW])
        c_ps = [ps(f"c_ps{i}", [P, 2 * CW]) for i in range(2)]
        work = [ps(f"work{i}", [P, T]) for i in range(2)]

        ld_cond, ld_gdn, ld_gup, ld_dp, ld_up, ld_vl, ld_bp = [sem("ld_" + n) for n in
                                                             ("cond", "gdn", "gup", "dp", "up", "vl", "bp")]
        ld_wo, ld_wdec, ld_bdec, ld_v, ld_gate, ld_ex = [sem("ld_" + n) for n in
                                                         ("wo", "wdec", "bdec", "v", "gate", "ex")]
        ld_x = [sem(f"ld_x{b}") for b in range(B)]
        v_zero = sem("v_zero")
        ident_ready = sem("ident_ready")
        consts = sem("consts")
        rootc_ready = sem("rootc_ready")
        cond_ready = sem("cond_ready")
        wdn_ready = sem("wdn_ready")
        wup_ready = sem("wup_ready")
        filled = sem("filled")
        emptied = [sem(f"emptied{i}") for i in range(2)]
        logit_ready = sem("logit_ready")
        sign_ready = sem("sign_ready")
        feat_ready = sem("feat_ready")
        stacked = [sem(f"stacked{b}") for b in range(B)]
        halves_ready = sem("halves_ready")
        scored = sem("scored")
        exped = sem("exped")
        masked = sem("masked")
        summed = sem("summed")
        added = sem("added")
        closed = sem("closed")
        ctx_ready = sem("ctx_ready")
        u_rows = sem("u_rows")
        u_stored = sem("u_stored")
        u_moved = sem("u_moved")
        u_ready = sem("u_ready")
        zo_ready = sem("zo_ready")
        chain_v = sem("chain_v")
        chain_p = sem("chain_p")
        stored = sem("stored")

        def full(eng, step):
            eng.wait_ge(filled, WORK[step] + 1)

        def done(eng, step):
            eng.wait_ge(emptied[WORK[step] % 2], WORK[step] // 2 + 1)

        def bank(step):
            return work[WORK[step] % 2]

        def empty(step):
            return emptied[WORK[step] % 2]

        block = ctx.enter_context(nc.Block())

        @block.sync
        def _(sp):
            sp.dma_start(cond_nat[:], cond).then_inc(ld_cond, 16)
            sp.dma_start(gam_dn[:, 0:HD], down_gamma).then_inc(ld_gdn, 16)
            sp.dma_start(gam_dn[:, HD:2 * HD], down_beta).then_inc(ld_gdn, 16)
            sp.dma_start(x_nat[:, 0], x[0].rearrange("(t p) d -> p t d", p=P)).then_inc(ld_x[0], 16)
            sp.dma_start(w_vl[:, :, 0:D], Wv.rearrange("(c p) n -> p c n", p=P)).then_inc(ld_vl, 16)
            sp.dma_start(w_vl[:, :, D:], Wp.rearrange("(c p) n -> p c n", p=P)).then_inc(ld_vl, 16)
            sp.dma_start(x_nat[:, 1], x[1].rearrange("(t p) d -> p t d", p=P)).then_inc(ld_x[1], 16)
            sp.dma_start(wdec[:], W_dec).then_inc(ld_wdec, 16)
            sp.dma_start(ex_nat[:], expert_w.rearrange("e (c p) h -> p e c h", p=P)).then_inc(ld_ex, 16)
            for s in ORDER:
                if s[0] == "phi" and s[2] == NG - 1:
                    b = s[1]
                    sp.wait_ge(halves_ready, NG * (b + 1))
                    if b >= 2:
                        sp.wait_ge(scored, BU * (b - 1))
                    for q, pair in enumerate((0, 1, 3, 2)):
                        for h in range(HG):
                            sp.dma_start(st[NF * q:NF * (q + 1), b % 2, :, h, :],
                                         feat_h[NF * h:NF * (h + 1), :, T * pair:T * (pair + 2)]
                                         ).then_inc(stacked[b], 16)
                    if b + 2 < B:
                        sp.dma_start(x_nat[:, b + 2], x[b + 2].rearrange("(t p) d -> p t d", p=P)
                                     ).then_inc(ld_x[b + 2], 16)
                elif s == ("U", 3):
                    done(sp, s)
                    for j in range(4):
                        sp.dma_start(u_dram[:, U_COLS * j:U_COLS * (j + 1)], u_row[KP * j:KP * j + B, 0:U_COLS]
                                     ).then_inc(u_stored, 16)
                    sp.wait_ge(u_stored, 16 * 4)
                    for c in range(DC):
                        sp.dma_start(u_raw[:, c], u_dram[:, P * K * c:P * K * (c + 1)].rearrange(
                            "b (p k) -> p b k", k=K)).then_inc(u_moved, 16)
                elif s[0] == "out":
                    _, b, h = s
                    done(sp, s)
                    sp.dma_start(out[b, 2 * P * h:2 * P * (h + 1), :].rearrange("(t p) d -> p t d", p=P),
                                 x_nat[:, b, 2 * h:2 * h + 2, :]).then_inc(stored, 16)
            sp.wait_ge(stored, 16 * 2 * B)

        @block.gpsimd
        def _(pool):
            nc.gpsimd.memset(ident[:], 0.0).then_inc(chain_p, 1)
            pool.wait_ge(chain_p, 1)
            nc.gpsimd.affine_select(out=ident[:], in_=ident[:], compare_op=ALU.not_equal, fill=1.0, base=0,
                                    pattern=[[-1, P]], channel_multiplier=1).then_inc(ident_ready, 1)
            nc.gpsimd.memset(v4[:], 0.0).then_inc(v_zero, 1)
            for m in range(DEPTH + 1):
                lo, hi = (0, 1) if m == 0 else (2 ** (m - 1), 2 ** m)
                c = (2.0 ** (1 - max(m, 1)) - 2.0 ** -DEPTH) / DEPTH
                nc.gpsimd.memset(level[:, :, lo:hi], c ** 0.5)
            for e in range(E):
                nc.gpsimd.memset(rank8[:, :, e:e + 1], float(E - e))
            nc.gpsimd.memset(feat[:, :, 0:1], 1.0)
            nc.gpsimd.memset(ones[:], 1.0)
            nc.gpsimd.memset(q_bd[:], 0.0)
            nc.gpsimd.memset(u_w[:], 0.0)
            nc.gpsimd.memset(ub_row[:], 0.0).then_inc(consts, 1)
            links = 1
            for s in ORDER:
                if s == ("start",) or s[0] == "unit":
                    for u in (0, 1) if s == ("start",) else (s[1] + 2,):
                        if u < ALL and unit(u)[1][4]:
                            pool.wait_ge(exped, u + 1)
                            tri = prob[:, u % RING, :, 0:P]
                            nc.gpsimd.affine_select(out=tri, in_=tri, compare_op=ALU.is_ge, fill=0.0, base=0,
                                                    pattern=[[0, HG], [1, P]], channel_multiplier=-1
                                                    ).then_inc(masked, 1)
                elif s[0] == "VL" and s[2] == TT - 1:
                    b = s[1]
                    pool.wait_ge(sign_ready, b + 1)
                    if b >= 1:
                        full(pool, ("phi", b - 1, NG - 1))
                    nc.gpsimd.tensor_copy(feat[:, :, 1:2], sign[:, :, 0:1]).then_inc(chain_p, 1)
                    for i in range(1, DEPTH):
                        n = 2 ** i
                        links += 1
                        pool.wait_ge(chain_p, links)
                        nc.gpsimd.tensor_tensor(feat[:, :, n:2 * n], feat[:, :, 0:n],
                                                sign[:, :, i:i + 1].broadcast_to([P, TT * H, n]), ALU.mult
                                                ).then_inc(feat_ready if i == DEPTH - 1 else chain_p, 1)
                elif s[0] == "zs":
                    done(pool, s)
                    for t in s[2]:
                        ins = nc.gpsimd.tensor_tensor(zo[:, t], z_nat[:, t:t + 1, :].broadcast_to([P, E, KP]),
                                                      pick[:, t, :].unsqueeze(2).broadcast_to([P, E, KP]), ALU.mult)
                    ins.then_inc(zo_ready, 1)

        @block.scalar
        def _(act):
            act.dma_start(gam_up[:, 0:D], up_gamma).then_inc(ld_gup, 16)
            act.dma_start(gam_up[:, D:2 * D], up_beta).then_inc(ld_gup, 16)
            act.dma_start(dproj[:], down_project.rearrange("(c p) n -> p c n", p=P)).then_inc(ld_dp, 16)
            act.dma_start(uproj[0:HD, :], up_project).then_inc(ld_up, 16)
            act.dma_start(uproj[HD:2 * HD, :], up_project).then_inc(ld_up, 16)
            act.dma_start(bp_b[:], bp.rearrange("(a n) -> a n", a=1).broadcast_to([P, H * DEPTH])
                          ).then_inc(ld_bp, 16)
            act.dma_start(wo[:], Wo.rearrange("(c p) n -> p c n", p=P)).then_inc(ld_wo, 16)
            act.wait_ge(v_zero, 1)
            for j in range(4):
                act.dma_start(v4[KP * j:KP * j + K, :], V).then_inc(ld_v, 16)
            act.dma_start(gate[:], gate_w).then_inc(ld_gate, 16)
            act.dma_start(bdec[:], b_dec[0:D * K].rearrange("(c p k) -> p c k", p=P, k=K)).then_inc(ld_bdec, 16)
            act.dma_start(bdec_row[:], b_dec[D * K:].rearrange("(a k) -> a k", a=1).broadcast_to([B, K])
                          ).then_inc(ld_bdec, 16)
            for s in ORDER:
                if s == ("start",) or s[0] == "unit":
                    for u in (0, 1) if s == ("start",) else (s[1] + 2,):
                        if u < ALL:
                            n = unit(u)[1][3]
                            act.wait_ge(scored, u + 1)
                            if u >= RING:
                                act.wait_ge(summed, u - RING + 1)
                                if adds(u - RING + 1):
                                    act.wait_ge(added, adds(u - RING + (place(u - RING)[1] == 0)))
                            nc.scalar.activation(prob[:, u % RING, :, 0:n], s_ps[:, u % 2, :, 0:n],
                                                 ACT.Exp).then_inc(exped, 1)
                elif s[0] == "xT":
                    full(act, s)
                    nc.scalar.copy(x_t[:, s[1] % 3, s[2], :], bank(s)[:]).then_inc(empty(s), 1)
                elif s[0] == "VL":
                    _, b, t = s
                    full(act, s)
                    act.wait_ge(logit_ready, TT * b + t + 1)
                    nc.scalar.copy(v_sb[:, b % 2, t, :], bank(s)[:, 0:D]).then_inc(empty(s), 1)
                    if t == TT - 1:
                        if b >= 1:
                            act.wait_ge(feat_ready, b)
                        nc.scalar.activation(sign[:], logit[:].rearrange("p t (h l) -> p (t h) l", l=DEPTH),
                                             ACT.Tanh, scale=0.5).then_inc(sign_ready, 1)
                elif s[0] == "wT":
                    full(act, s)
                    nc.scalar.copy(wt[:], bank(s)[:, 0:DC * (P + E)]).then_inc(empty(s), 1)
                elif s[0] == "woT":
                    full(act, s)
                    nc.scalar.copy(wo_t[:].rearrange("p c n -> p (c n)"), bank(s)[:]).then_inc(empty(s), 1)
                elif s[0] == "eT":
                    full(act, s)
                    nc.scalar.copy(ex_t[:, s[1]].rearrange("p c n -> p (c n)"), bank(s)[:]).then_inc(empty(s), 1)
                elif s[0] == "zoT":
                    full(act, s)
                    nc.scalar.copy(zo_t[:, :, CW * s[2]:CW * (s[2] + 1)], bank(s)[:].rearrange("p (e t) -> p e t", e=2)
                                   ).then_inc(empty(s), 1)

        @block.vector
        def _(dve):
            links = [0]

            def link(ins):
                links[0] += 1
                ins.then_inc(chain_v, 1)
                dve.wait_ge(chain_v, links[0])

            def normalise(m):
                b, g, half = m // BC, m % NG, m % BC // NG
                if m >= 1:
                    dve.wait_ge(ctx_ready, m)
                link(nc.vector.reciprocal(rden[:], c_ps[m % 2][:, CW:2 * CW]))
                nc.vector.tensor_tensor(ctx_t[:, b % 2, g, CW * half:CW * (half + 1)], c_ps[m % 2][:, 0:CW], rden[:],
                                        ALU.mult).then_inc(ctx_ready, 1)

            dve.wait_ge(consts, 1)
            dve.wait_ge(ident_ready, 1)
            link(nc.vector.tensor_tensor(level_d[:], level[:].rearrange("p h f -> p (h f)"), ident[:], ALU.mult))
            nc.vector.reduce_sum(rootc[:], level_d[:], AX_X).then_inc(rootc_ready, 1)
            nc.vector.memset(cond_c[:], 0.0)
            for s in ORDER:
                kind = s[0]
                if kind == "cond":
                    full(dve, s)
                    link(nc.vector.tensor_copy(cond_b[:], bank(s)[:, 0:B].unsqueeze(2).broadcast_to([P, B, P])))
                    nc.vector.tensor_copy(cond_c[:, 0:B], bank(s)[:, 0:B]).then_inc(empty(s), 1)
                elif kind == "gdn":
                    g = bank(s)[:].rearrange("p (b n) -> p b n", b=B)
                    dve.wait_ge(ld_dp, 16)
                    full(dve, s)
                    for b in range(B):
                        w3 = w_tmp[:].rearrange("p (b c n) -> p b c n", b=B, c=DC)
                        ins = nc.vector.tensor_tensor(w3[:, b], dproj[:],
                                                      g[:, b:b + 1, 0:HD].broadcast_to([P, DC, HD]), ALU.mult)
                    link(ins)
                    for b in range(B):
                        ins = nc.vector.tensor_tensor(w_dn[:, b], w3[:, b],
                                                      g[:, b:b + 1, HD:2 * HD].broadcast_to([P, DC, HD]), ALU.add)
                    ins.then_inc(empty(s), 1)
                elif kind == "gup":
                    b = s[1]
                    dve.wait_ge(ld_up, 32)
                    full(dve, s)
                    link(nc.vector.tensor_tensor(u_tmp[:], uproj[:], bank(s)[:, 0:D], ALU.mult))
                    nc.vector.tensor_tensor(w_up[:, b, :], u_tmp[:], bank(s)[:, D:2 * D], ALU.add
                                            ).then_inc(empty(s), 1)
                elif kind == "down":
                    full(dve, s)
                    nc.vector.tensor_scalar(act_t[:], bank(s)[:, 0:T // 2], 0.0, None, ALU.max
                                            ).then_inc(empty(s), 1)
                elif kind == "up":
                    _, b, j = s
                    full(dve, s)
                    half = slice(T // 2 * j, T // 2 * (j + 1))
                    nc.vector.tensor_tensor(h_t[:, :, half], bank(s)[:].rearrange("p (c t) -> p c t", c=DC),
                                            x_t[:, b % 3, :, half], ALU.add).then_inc(empty(s), 1)
                elif kind == "VL":
                    _, b, t = s
                    if t == 0:
                        dve.wait_ge(ld_bp, 16)
                        if b >= 1:
                            dve.wait_ge(sign_ready, b)
                    full(dve, s)
                    nc.vector.tensor_tensor(logit[:, t, :], bank(s)[:, D:D + H * DEPTH], bp_b[:], ALU.add
                                            ).then_inc(logit_ready, 1)
                elif kind == "phi":
                    _, b, g = s
                    dve.wait_ge(rootc_ready, 1)
                    full(dve, s)
                    if b >= 1:
                        dve.wait_ge(stacked[b - 1], 16 * 4 * HG)
                    slots = feat_h[:, g, :].rearrange("p (n t) -> p n t", t=T)
                    link(nc.vector.tensor_scalar(slots[:, 0, :], bank(s)[:], rootc[:], None, ALU.mult))
                    nc.vector.scalar_tensor_tensor(out=slots[:, 2, :], in0=bank(s)[:], scalar=rootc[:],
                                                   in1=slots[:, 0, :], op0=ALU.mult, op1=ALU.subtract
                                                   ).then_inc(empty(s), 1)
                    nc.vector.tensor_copy(slots[:, 1, :], slots[:, 0, :])
                    nc.vector.tensor_copy(slots[:, 4, :], slots[:, 0, :])
                    done(dve, s)
                    nc.vector.tensor_copy(slots[:, 3, :], slots[:, 2, :]).then_inc(halves_ready, 1)
                elif kind == "Q":
                    full(dve, s)
                    for j in range(TT):
                        ins = nc.vector.tensor_copy(q_bd[KP * j:KP * j + KP, j, :], bank(s)[KP * j:KP * j + KP, 0:E])
                    ins.then_inc(empty(s), 1)
                elif kind == "U":
                    m = s[1]
                    if m == 3:
                        dve.wait_ge(ld_bdec, 32)
                        full(dve, s)
                        nc.vector.tensor_tensor(ub_row[:, :, 0:K],
                                                bank(s)[0:B, U_PIECE:U_PIECE + K].unsqueeze(1).broadcast_to([B, TT, K]),
                                                bdec_row[:].unsqueeze(1).broadcast_to([B, TT, K]), ALU.add)
                    full(dve, s)
                    nc.vector.tensor_copy(u_row[:, U_PIECE * m:U_PIECE * (m + 1)], bank(s)[:, 0:U_PIECE]
                                          ).then_inc(empty(s), 1)
                elif kind == "ubT":
                    full(dve, s)
                    nc.vector.tensor_copy(ub_col[:], bank(s)[:, 0:B]).then_inc(empty(s), 1)
                elif kind == "Uadd":
                    dve.wait_ge(u_moved, 16 * DC)
                    for c in range(DC):
                        ins = nc.vector.tensor_tensor(u_w[:, c, :, 0:K], u_raw[:, c],
                                                      bdec[:, c:c + 1, :].broadcast_to([P, B, K]), ALU.add)
                    ins.then_inc(u_ready, 1)
                elif kind == "WoU":
                    full(dve, s)
                    nc.vector.tensor_copy(wo_u[:].rearrange("p c n -> p (c n)"), bank(s)[:, 0:DC * P]
                                          ).then_inc(empty(s), 1)
                elif kind == "G":
                    full(dve, s)
                    nc.vector.tensor_tensor(gexp[:, s[1], :], bank(s)[:, 0:D], v4[:], ALU.add
                                            ).then_inc(empty(s), 1)
                elif kind == "start":
                    pass
                elif kind == "unit":
                    u = s[1]
                    m, i = place(u)
                    if not long(m) and unit(u)[1][5]:
                        dve.wait_ge(summed, u + 1)
                        normalise(m)
                    v = u + 1
                    if v < ALL and long(place(v)[0]) and place(v)[1] > 0:
                        m, i = place(v)
                        _, (_, _, _, n, diagonal, _) = unit(v)
                        dve.wait_ge(exped, v + 1)
                        if diagonal:
                            dve.wait_ge(masked, diagonals(v))
                        if i > 1:
                            dve.wait_ge(added, adds(v) - 1)
                        acc = tiles[:, m % 2, :, CW - n:CW]
                        other = prob[:, (v - 1) % RING, :, 0:n] if i == 1 else acc
                        nc.vector.tensor_tensor(acc, other, prob[:, v % RING, :, 0:n], ALU.add).then_inc(added, 1)
                elif kind == "den":
                    dve.wait_ge(closed, longs(s[1]))
                    normalise(s[1])
                elif kind == "zT":
                    _, b, ts = s
                    rows = slice(KP * ts[0], KP * (ts[-1] + 1))
                    full(dve, s)
                    nc.vector.tensor_scalar(z_t[rows, :], bank(s)[rows, 0:P], ub_col[rows, b:b + 1], None, ALU.add
                                            ).then_inc(empty(s), 1)
                elif kind == "zs":
                    _, b, ts = s
                    nt = len(ts)
                    span = slice(ts[0], ts[-1] + 1)
                    sc = bank(s)[:, P:P + nt * E].rearrange("p (t e) -> p t e", e=E)
                    full(dve, s)
                    if b >= 1:
                        dve.wait_ge(zo_ready, b + (ts == SECOND))
                    nc.vector.tensor_copy(z_nat[:, span, :].rearrange("p t k -> p (t k)"), bank(s)[:, 0:KP * nt])
                    link(nc.vector.reduce_max(smax[:, span], sc, AX_X))
                    link(nc.vector.tensor_tensor(hit[:, span], sc,
                                                 smax[:, span].unsqueeze(2).broadcast_to([P, nt, E]), ALU.is_ge))
                    link(nc.vector.tensor_tensor(key[:, span], hit[:, span], rank8[:, span], ALU.mult))
                    link(nc.vector.reduce_max(kmax[:, span], key[:, span], AX_X))
                    nc.vector.tensor_tensor(pick[:, span], key[:, span],
                                            kmax[:, span].unsqueeze(2).broadcast_to([P, nt, E]),
                                            ALU.is_equal).then_inc(empty(s), 1)
                elif kind == "out":
                    _, b, h = s
                    full(dve, s)
                    xs = x_nat[:, b, 2 * h:2 * h + 2, :]
                    nc.vector.tensor_tensor(xs, bank(s)[:].rearrange("p (t d) -> p t d", t=2), xs, ALU.add
                                            ).then_inc(empty(s), 1)

        @block.tensor
        def _(pe):
            def mm(o, w, r, start=True, stop=True):
                return nc.tensor.matmul(o, w, r, start=start, stop=stop, skip_group_check=True)

            def scores(u):
                b, (g, kt, q0, n, _, _) = unit(u)
                if u % BU == 0:
                    pe.wait_ge(stacked[b], 16 * 4 * HG)
                if u >= 2:
                    pe.wait_ge(exped, u - 1)
                for h in range(HG):
                    ins = mm(s_ps[:, u % 2, h, 0:n],
                             st[:, b % 2, g, h, P * kt:P * (kt + 1)], st[:, b % 2, g, h, T + q0:T + q0 + n])
                ins.then_inc(scored, 1)

            def context(u):
                b, (g, kt, q0, n, diagonal, last) = unit(u)
                m, _ = place(u)
                if diagonal:
                    pe.wait_ge(masked, diagonals(u))
                pe.wait_ge(exped, u + 1)
                if kt == 0:
                    if m >= 2:
                        pe.wait_ge(ctx_ready, m - 1)
                    if u % BU == 0:
                        done(pe, ("VL", b, TT - 1))
                lo = q0 % CW
                for h in range(HG):
                    ins = mm(c_ps[m % 2][DH * h:DH * (h + 1), lo:lo + n],
                             v_sb[:, b % 2, kt, DH * (HG * g + h):DH * (HG * g + h + 1)], prob[:, u % RING, h, 0:n],
                             start=(kt == 0), stop=last)
                if not long(m):
                    for h in range(HG):
                        ins = mm(c_ps[m % 2][DH * h:DH * (h + 1), CW + lo:CW + lo + n], ones[:],
                                 prob[:, u % RING, h, 0:n], start=False, stop=last)
                ins.then_inc(summed, 1)

            def denominators(m):
                pe.wait_ge(added, (LONG - 1) * longs(m))
                for h in range(HG):
                    ins = mm(c_ps[m % 2][DH * h:DH * (h + 1), CW:2 * CW], ones[:], tiles[:, m % 2, h, :], start=False)
                ins.then_inc(closed, 1)

            pe.wait_ge(ident_ready, 1)
            for s in ORDER:
                kind = s[0]
                if kind == "start":
                    pe.wait_ge(consts, 1)
                    scores(0)
                    scores(1)
                    continue
                if kind == "unit":
                    context(s[1])
                    if s[1] + 2 < ALL:
                        scores(s[1] + 2)
                    continue
                if kind == "den":
                    denominators(s[1])
                    continue
                if kind == "Uadd":
                    continue
                n = WORK[s]
                o = bank(s)
                if n >= 2:
                    pe.wait_ge(emptied[n % 2], n // 2)
                if kind == "cond":
                    pe.wait_ge(ld_cond, 16)
                    ins = nc.tensor.transpose(o[:, 0:B], cond_nat[:], ident[0:B, 0:B])
                elif kind == "gdn":
                    done(pe, ("cond",))
                    pe.wait_ge(ld_gdn, 32)
                    for b in range(B):
                        ins = mm(o[:, P * b:P * (b + 1)], cond_b[:, b, :], gam_dn[:])
                elif kind == "gup":
                    if s[1] == 0:
                        pe.wait_ge(ld_gup, 32)
                    ins = mm(o[:], cond_b[:, s[1], :], gam_up[:])
                elif kind == "xT":
                    _, b, c = s
                    if c == 0:
                        pe.wait_ge(ld_x[b], 16)
                    for t in range(TT):
                        ins = nc.tensor.transpose(o[:, P * t:P * (t + 1)], x_nat[:, b, t, P * c:P * (c + 1)], ident[:])
                elif kind == "down":
                    b = s[1]
                    if b == 0:
                        done(pe, ("gdn",))
                    for c in range(DC):
                        done(pe, ("xT", b, c))
                    for c in range(DC):
                        for j in range(2):
                            ins = mm(o[HD * j:HD * (j + 1), 0:T // 2], w_dn[:, b, c, :],
                                     x_t[:, b % 3, c, T // 2 * j:T // 2 * (j + 1)], start=(c == 0), stop=(c == DC - 1))
                elif kind == "up":
                    _, b, j = s
                    if j == 0:
                        done(pe, ("gup", b))
                        done(pe, ("down", b))
                    for c in range(DC):
                        ins = mm(o[:, T // 2 * c:T // 2 * (c + 1)], w_up[HD * j:HD * (j + 1), b, P * c:P * (c + 1)],
                                 act_t[HD * j:HD * (j + 1), :])
                elif kind == "VL":
                    _, b, t = s
                    if t == 0:
                        if b == 0:
                            pe.wait_ge(ld_vl, 32)
                        done(pe, ("up", b, 0))
                        done(pe, ("up", b, 1))
                    for c in range(DC):
                        ins = mm(o[:, 0:D + H * DEPTH], h_t[:, c, P * t:P * (t + 1)], w_vl[:, c, :],
                                 start=(c == 0), stop=(c == DC - 1))
                elif kind == "phi":
                    _, b, g = s
                    pe.wait_ge(feat_ready, b + 1)
                    for t in range(TT):
                        ins = nc.tensor.transpose(
                            o[:, P * t:P * (t + 1)],
                            feat[:, H * t + HG * g:H * t + HG * (g + 1), :].rearrange("p h f -> p (h f)"), ident[:])
                elif kind == "wT":
                    pe.wait_ge(ld_v, 16 * 4)
                    pe.wait_ge(ld_gate, 16)
                    for c in range(DC):
                        nc.tensor.transpose(o[:, P * c:P * (c + 1)], v4[:, P * c:P * (c + 1)], ident[:])
                        ins = nc.tensor.transpose(o[:, DC * P + E * c:DC * P + E * (c + 1)],
                                                  gate[:, P * c:P * (c + 1)], ident[0:E, 0:E])
                elif kind == "woT":
                    pe.wait_ge(ld_wo, 16)
                    for d in range(DC):
                        for c in range(DC):
                            ins = nc.tensor.transpose(o[:, D * d + P * c:D * d + P * (c + 1)],
                                                      wo[:, c, P * d:P * (d + 1)], ident[:])
                elif kind == "Q":
                    done(pe, ("wT",))
                    for c in range(DC):
                        ins = mm(o[:, 0:E], wt[:, P * c:P * (c + 1)], wt[:, DC * P + E * c:DC * P + E * (c + 1)],
                                 start=(c == 0), stop=(c == DC - 1))
                elif kind == "U":
                    m = s[1]
                    if m == 0:
                        pe.wait_ge(ld_wdec, 16)
                    for j in range(4):
                        lo = U_COLS * j + U_PIECE * m
                        ins = mm(o[KP * j:KP * (j + 1), 0:U_PIECE], cond_c[:], wdec[:, lo:lo + U_PIECE])
                    if m == 3:
                        ins = mm(o[0:KP, U_PIECE:U_PIECE + K], cond_c[:], wdec[:, D * K:(D + 1) * K])
                elif kind == "ubT":
                    done(pe, ("U", 3))
                    ins = nc.tensor.transpose(o[:, 0:B], ub_row[:].rearrange("b j k -> b (j k)"), ident[0:B, 0:B])
                elif kind == "WoU":
                    pe.wait_ge(u_ready, 1)
                    done(pe, ("woT",))
                    for c in range(DC):
                        for d in range(DC):
                            ins = mm(o[:, P * c:P * (c + 1)], wo_t[:, d, P * c:P * (c + 1)],
                                     u_w[:, d].rearrange("p b k -> p (b k)"), start=(d == 0), stop=(d == DC - 1))
                elif kind == "eT":
                    e = s[1]
                    if e == 0:
                        pe.wait_ge(ld_ex, 16)
                    for hc in range(DC):
                        for fc in range(DC):
                            ins = nc.tensor.transpose(o[:, D * hc + P * fc:D * hc + P * (fc + 1)],
                                                      ex_nat[:, e, fc, P * hc:P * (hc + 1)], ident[:])
                elif kind == "G":
                    for e in range(4):
                        done(pe, ("eT", 4 * s[1] + e))
                    for hc in range(DC):
                        for j in range(4):
                            ins = mm(o[KP * j:KP * (j + 1), 0:D], wt[:, P * hc:P * hc + KP],
                                     ex_t[:, 4 * s[1] + j, hc, :], start=(hc == 0), stop=(hc == DC - 1))
                elif kind == "zT":
                    _, b, ts = s
                    if b == 0:
                        done(pe, ("ubT",))
                        done(pe, ("WoU",))
                    pe.wait_ge(ctx_ready, BC * b + (NG if ts == FIRST else BC))
                    for c in range(2 * DC):
                        for t in ts:
                            tok = slice(P * t, P * (t + 1))
                            w = u_w[:, c, b, :] if c < DC else wo_u[:, c - DC, KP * b:KP * (b + 1)]
                            r = x_t[:, b % 3, c, tok] if c < DC else ctx_t[:, b % 2, c - DC, tok]
                            ins = mm(o[KP * t:KP * (t + 1), 0:P], w, r, start=(c == 0), stop=(c == 2 * DC - 1))
                elif kind == "zs":
                    _, b, ts = s
                    done(pe, ("zT", b, ts))
                    if b == 0:
                        done(pe, ("Q",))
                    rows = slice(KP * ts[0], KP * (ts[-1] + 1))
                    nc.tensor.transpose(o[:, 0:KP * len(ts)], z_t[rows, :], ident[rows, rows])
                    ins = mm(o[:, P:P + len(ts) * E], z_t[rows, :],
                             q_bd[rows, ts[0]:ts[-1] + 1].rearrange("p t e -> p (t e)"))
                elif kind == "zoT":
                    _, b, hf = s
                    pe.wait_ge(zo_ready, b + 1 + (b == B - 1 and hf == 1))
                    for e in range(2):
                        for i in range(2):
                            ins = nc.tensor.transpose(
                                o[:, CW * e + P * i:CW * e + P * (i + 1)],
                                zo[:, 2 * hf + i, 4 * e:4 * e + 4, :].rearrange("p e k -> p (e k)"), ident[:])
                elif kind == "out":
                    _, b, hf = s
                    if b == 0 and hf == 0:
                        done(pe, ("G", 0))
                        done(pe, ("G", 1))
                    for c in range(2 * DC):
                        if c == DC:
                            done(pe, ("zoT", b, hf))
                        for i in range(2):
                            tok = slice(P * (2 * hf + i), P * (2 * hf + i + 1))
                            w = ctx_t[:, b % 2, c, tok] if c < DC else zo_t[:, c - DC, tok]
                            r = wo[:, c, :] if c < DC else gexp[:, c - DC, :]
                            ins = mm(o[:, D * i:D * (i + 1)], w, r, start=(c == 0 and i == 0), stop=(c == 2 * DC - 1))
                ins.then_inc(filled, 1)


NAMES = ["x", "cond_512", "L0_cond_down_project", "L0_cond_down_gamma", "L0_cond_down_beta", "L0_cond_up_project",
         "L0_cond_up_gamma", "L0_cond_up_beta", "L0_attn_Wp", "L0_attn_bp", "L0_attn_Wv", "L0_attn_Wo",
         "L0_cond2_W_dec", "L0_cond2_b_dec", "L0_cond2_V", "L0_ffn_gate_w", "L0_ffn_expert_w"]


def kernel(**inputs):
    import numpy as np
    import concourse.bacc as bacc
    from concourse.bass_utils import run_bass_kernel_spmd as run

    nc = bacc.Bacc("TRN2", target_bir_lowering=False, num_devices=1)
    arrays, args = {}, []
    for name in NAMES:
        a = np.ascontiguousarray(inputs[name])
        arrays["in_" + name] = a
        args.append(nc.dram_tensor("in_" + name, a.shape, mybir.dt.from_np(a.dtype), kind="ExternalInput").ap())
    args.append(nc.dram_tensor("out_x", (B, T, D), F32, kind="ExternalOutput").ap())
    build(nc, *args)
    return run(nc, [arrays], core_ids=[0]).results[0]["out_x"]
```

```python
from contextlib import ExitStack

import concourse.bass as bass
from concourse import mybir

F32 = mybir.dt.float32
F16 = mybir.dt.float16
ALU = mybir.AluOpType
ACT = mybir.ActivationFunctionType
AX_X = mybir.AxisListType.X

P = 128
B, T, D = 4, 512, 256
TT = T // P
DC = D // P
HD = 64
H, DEPTH = 8, 5
DH = D // H
NF = 2 ** DEPTH
HG = 4
NG = H // HG
K = 30
KP = 32
E = 8
CW = 2 * P
U_COLS = D * K // 4
U_PIECE = U_COLS // 4

UNITS = [(g, *u) for chunk in (((0, 0, 256, True, False), (1, 128, 128, True, True)),
                               ((0, 256, 256, False, False), (1, 256, 256, False, False), (2, 256, 256, True, False),
                                (3, 384, 128, True, True))) for g in range(NG) for u in chunk]
BU = len(UNITS)
ALL = B * BU
BC = 2 * NG
RING = 4
LONG = 4


def unit(u):
    return u // BU, UNITS[u % BU]


def diagonals(u):
    return sum(unit(i)[1][4] for i in range(u + 1))


def chunks(u):
    return sum(unit(i)[1][5] for i in range(u + 1))


def place(u):
    first = u
    while first % BU and not unit(first - 1)[1][5]:
        first -= 1
    return chunks(u) - unit(u)[1][5], u - first


def long(m):
    return m % BC >= NG


def longs(m):
    return sum(long(i) for i in range(m + 1))


def adds(u):
    return sum(long(place(i)[0]) and place(i)[1] > 0 for i in range(min(u + 1, ALL)))


ALL_T, FIRST, SECOND = (0, 1, 2, 3), (0, 1), (2, 3)
PROLOGUE = [("cond",), ("xT", 0, 0), ("xT", 0, 1), ("gdn", (0,)), ("gup", 0), ("down", 0), ("gup", 1), ("up", 0, 0),
            ("up", 0, 1),
            ("VL", 0, 0), ("VL", 0, 1), ("VL", 0, 2), ("VL", 0, 3), ("feat", 0), ("xT", 1, 0), ("xT", 1, 1),
            ("gup", 2), ("gdn", (1, 2, 3)), ("phi", 0, 0), ("phi", 0, 1), ("down", 1), ("gup", 3), ("up", 1, 0),
            ("up", 1, 1), ("VL", 1, 0), ("U", 0), ("VL", 1, 1), ("U", 1), ("wT",), ("VL", 1, 2), ("U", 2), ("woT",),
            ("VL", 1, 3), ("U", 3), ("Q",), ("feat", 1), ("eT", 0), ("eT", 1), ("start",)]


def between(b):
    n1, n2, prv = b + 1, b + 2, b - 1
    gaps = [[] for _ in range(BU)]
    if n2 < B:
        gaps[0] += [("xT", n2, 0)]
        gaps[1] += [("xT", n2, 1)]
    if n1 < B:
        gaps[0] += [("phi", n1, 0)]
        gaps[1] += [("phi", n1, 1)]
    if b == 0:
        gaps[0] += [("eT", 4)]
        gaps[1] += [("G", 0)]
        gaps[2] += [("ubT",)]
        gaps[3] += [("eT", 5)]
        gaps[5] += [("eT", 6), ("Uadd",)]
        gaps[6] += [("WoU",), ("eT", 7)]
        gaps[9] += [("G", 1)]
    if prv >= 1:
        gaps[0] += [("out", prv - 1, 3)]
    if prv >= 0:
        gaps[2] += [("zT", prv, ALL_T)]
        gaps[3] += [("zs", prv, ALL_T)]
        gaps[4] += [("zo", prv, 0)]
        gaps[5] += [("zo", prv, 1)]
    if n2 < B:
        gaps[3] += [("down", n2)]
        gaps[4] += [("up", n2, 0)]
        gaps[5] += [("up", n2, 1)]
        gaps[6] += [("VL", n2, 0)]
        gaps[8] += [("VL", n2, 1)]
        gaps[10] += [("VL", n2, 2), ("VL", n2, 3)]
        gaps[11] += [("feat", n2)]
    if prv >= 0:
        gaps[6] += [("zoT", prv, 0)]
        gaps[7] += [("out", prv, 0), ("zoT", prv, 1)]
        gaps[9] += [("out", prv, 1)]
        gaps[11 if n2 < B else 10] += [("out", prv, 2)]
    if b == B - 1:
        gaps[7] += [("zT", b, FIRST)]
        gaps[8] += [("zs", b, FIRST), ("zo", b, 0)]
        gaps[11] += [("out", prv, 3), ("zoT", b, 0)]
    return gaps


ORDER = PROLOGUE + [("eT", 2), ("eT", 3)]
_open = []
for _b in range(B):
    for _i, _gap in enumerate(between(_b)):
        _u = _b * BU + _i
        ORDER += [("unit", _u)] + _open
        _m = place(_u)[0]
        _open = [("den", _m)] if UNITS[_i][5] and long(_m) else []
        ORDER += _gap
ORDER += _open + [("out", B - 1, 0), ("zT", B - 1, SECOND), ("zs", B - 1, SECOND), ("zo", B - 1, 1),
                  ("out", B - 1, 1), ("zoT", B - 1, 1), ("out", B - 1, 2), ("out", B - 1, 3)]
NO_BANK = ("unit", "den", "start", "Uadd", "feat", "zo")
EARLY = 6
WORK, _turns = {}, [0] * EARLY
for _n, _s in enumerate(s for s in ORDER if s[0] not in NO_BANK):
    _k = _n % (EARLY if _s in PROLOGUE else 2)
    WORK[_s] = (_n, _k, _turns[_k])
    _turns[_k] += 1
EARLY_TURNS = [1 + max(turn for _, k, turn in WORK.values() if k == i) for i in range(EARLY)]


def build(nc, x, cond, down_project, down_gamma, down_beta, up_project, up_gamma, up_beta, Wp, bp, Wv, Wo,
          W_dec, b_dec, V, gate_w, expert_w, out):
    with ExitStack() as ctx:
        def sb(name, shape, dt=F32):
            return ctx.enter_context(nc.sbuf_tensor(name, shape, dt))

        def ps(name, shape, dt=F32):
            return ctx.enter_context(nc.psum_tensor(name, shape, dt))

        def sem(name):
            return ctx.enter_context(nc.semaphore(name))

        x_nat = sb("x_nat", [P, B, TT, D])
        cond_nat = sb("cond_nat", [B, P])
        gam_dn = sb("gam_dn", [P, 2 * HD])
        gam_up = sb("gam_up", [P, 2 * D])
        dproj = sb("dproj", [P, DC, HD])
        uproj = sb("uproj", [P, D])
        w_vl = sb("w_vl", [P, DC, D + H * DEPTH])
        bp_b = sb("bp_b", [P, H * DEPTH])
        wo = sb("wo", [P, DC, D])
        wdec = sb("wdec", [P, (D + 1) * K])
        bdec = sb("bdec", [P, DC, K])
        bdec_row = sb("bdec_row", [B, K])
        v4 = sb("v4", [P, D])
        gate = sb("gate", [E, D])
        ex_nat = sb("ex_nat", [P, E, DC, D])
        ident = sb("ident", [P, P])
        level = sb("level", [P, HG, NF])
        level_d = sb("level_d", [P, HG * NF])
        rootc = sb("rootc", [P, 1])
        ones = sb("ones", [P, DH])
        rank8 = sb("rank8", [P, TT, E])
        cond_b = sb("cond_b", [P, B, P])
        cond_c = sb("cond_c", [P, KP])
        w_dn = sb("w_dn", [P, B, DC, HD])
        w_up = sb("w_up", [P, B, D])
        u_row = sb("u_row", [P, U_COLS + K])
        u_raw = sb("u_raw", [P, DC, B, K])
        u_w = sb("u_w", [P, DC, B, KP])
        ub_row = sb("ub_row", [B, TT, KP])
        ub_col = sb("ub_col", [P, B])
        wt = sb("wt", [P, DC * P + DC * E])
        wo_t = sb("wo_t", [P, DC, D])
        wo_u = sb("wo_u", [P, DC, B * KP])
        q_bd = sb("q_bd", [P, TT, E])
        ex_t = wdec[:, 0:E * DC * D].rearrange("p (e c f) -> p e c f", e=E, c=DC)
        tiles = wdec[:, E * DC * D:E * DC * D + 2 * HG * CW].rearrange("p (i h q) -> p i h q", i=2, h=HG)
        gexp = sb("gexp", [P, 2, D])
        x_t = sb("x_t", [P, B, DC, T])
        act_t = sb("act_t", [P, T // 2])
        h_t = sb("h_t", [P, DC, T])
        v_two = sb("v_two", [P, 2, TT, D])
        v_sb = [v_two[:, 0], v_two[:, 1], ex_nat[:, 0:2].rearrange("p e c d -> p (e c) d")]
        logit = sb("logit", [P, TT, H * DEPTH])
        sign = sb("sign", [P, TT * H, DEPTH])
        feat = sb("feat", [P, TT * H, NF])
        feat_h = sb("feat_h", [P, NG, 5 * T], F16)
        st = sb("st", [P, 2, NG, HG, 2 * T], F16)
        prob = sb("prob", [P, RING, HG, CW])
        rden = sb("rden", [P, CW])
        ctx_t = sb("ctx_t", [P, 2, NG, T])
        z_t = sb("z_t", [P, P])
        z_nat = sb("z_nat", [P, TT, KP])
        smax = sb("smax", [P, TT])
        kmax = sb("kmax", [P, TT])
        hit = sb("hit", [P, TT, E])
        key = sb("key", [P, TT, E])
        pick = sb("pick", [P, TT, E])
        zo = sb("zo", [P, TT, E, KP])
        zo_t = wdec[:, E * DC * D + 2 * HG * CW:E * DC * D + 2 * HG * CW + 2 * T].rearrange("p (c t) -> p c t", c=2)
        u_dram = nc.dram_tensor("u_scratch", (B, D * K), F32, kind="Internal").ap()
        s_ps = ps("s_ps", [P, 2, HG, CW])
        c_ps = [ps(f"c_ps{i}", [P, 2 * CW]) for i in range(2)]
        work = [ps(f"work{i}", [P, T]) for i in range(2)]
        work += [s_ps[:, i // 2, 2 * (i % 2):2 * (i % 2) + 2, :].rearrange("p h q -> p (h q)") for i in range(4)]

        ld_cond, ld_gdn, ld_gup, ld_dp, ld_up, ld_vl, ld_bp = [sem("ld_" + n) for n in
                                                             ("cond", "gdn", "gup", "dp", "up", "vl", "bp")]
        ld_wo, ld_wdec, ld_bdec, ld_v, ld_gate, ld_ex = [sem("ld_" + n) for n in
                                                         ("wo", "wdec", "bdec", "v", "gate", "ex")]
        ld_x = [sem(f"ld_x{b}") for b in range(B)]
        v_zero = sem("v_zero")
        ident_ready = sem("ident_ready")
        consts = sem("consts")
        rootc_ready = sem("rootc_ready")
        cond_ready = sem("cond_ready")
        wdn_ready = sem("wdn_ready")
        wup_ready = sem("wup_ready")
        filled = sem("filled")
        emptied = [sem(f"emptied{i}") for i in range(EARLY)]
        logit_ready = sem("logit_ready")
        sign_ready = sem("sign_ready")
        feat_ready = sem("feat_ready")
        stacked = [sem(f"stacked{b}") for b in range(B)]
        high_ready = sem("high_ready")
        copies_ready = sem("copies_ready")
        halves_ready = sem("halves_ready")
        scored = sem("scored")
        exped = sem("exped")
        masked = sem("masked")
        summed = sem("summed")
        added = sem("added")
        closed = sem("closed")
        ctx_ready = sem("ctx_ready")
        u_rows = sem("u_rows")
        u_stored = sem("u_stored")
        u_moved = sem("u_moved")
        u_ready = sem("u_ready")
        zo_ready = sem("zo_ready")
        chain_v = sem("chain_v")
        chain_p = sem("chain_p")
        stored = sem("stored")

        def full(eng, step):
            eng.wait_ge(filled, WORK[step][0] + 1)

        def done(eng, step):
            eng.wait_ge(emptied[WORK[step][1]], WORK[step][2] + 1)

        def bank(step):
            return work[WORK[step][1]]

        def empty(step):
            return emptied[WORK[step][1]]

        block = ctx.enter_context(nc.Block())

        @block.sync
        def _(sp):
            sp.dma_start(cond_nat[:], cond).then_inc(ld_cond, 16)
            sp.dma_start(x_nat[:, 0], x[0].rearrange("(t p) d -> p t d", p=P)).then_inc(ld_x[0], 16)
            sp.dma_start(gam_dn[:, 0:HD], down_gamma).then_inc(ld_gdn, 16)
            sp.dma_start(gam_dn[:, HD:2 * HD], down_beta).then_inc(ld_gdn, 16)
            sp.dma_start(w_vl[:, :, 0:D], Wv.rearrange("(c p) n -> p c n", p=P)).then_inc(ld_vl, 16)
            sp.dma_start(w_vl[:, :, D:], Wp.rearrange("(c p) n -> p c n", p=P)).then_inc(ld_vl, 16)
            sp.dma_start(x_nat[:, 1], x[1].rearrange("(t p) d -> p t d", p=P)).then_inc(ld_x[1], 16)
            sp.dma_start(wdec[:], W_dec).then_inc(ld_wdec, 16)
            sp.dma_start(ex_nat[:], expert_w.rearrange("e (c p) h -> p e c h", p=P)).then_inc(ld_ex, 16)
            for s in ORDER:
                if s[0] == "phi" and s[2] == NG - 1:
                    b = s[1]
                    sp.wait_ge(copies_ready, NG * (b + 1))
                    sp.wait_ge(halves_ready, NG * (b + 1))
                    if b >= 2:
                        sp.wait_ge(scored, BU * (b - 1))
                    for q, pair in enumerate((0, 1, 3, 2)):
                        for h in range(HG):
                            sp.dma_start(st[NF * q:NF * (q + 1), b % 2, :, h, :],
                                         feat_h[NF * h:NF * (h + 1), :, T * pair:T * (pair + 2)]
                                         ).then_inc(stacked[b], 16)
                    if b + 2 < B:
                        sp.dma_start(x_nat[:, b + 2], x[b + 2].rearrange("(t p) d -> p t d", p=P)
                                     ).then_inc(ld_x[b + 2], 16)
                elif s == ("U", 3):
                    done(sp, s)
                    for j in range(4):
                        sp.dma_start(u_dram[:, U_COLS * j:U_COLS * (j + 1)], u_row[KP * j:KP * j + B, 0:U_COLS]
                                     ).then_inc(u_stored, 16)
                    sp.wait_ge(u_stored, 16 * 4)
                    for c in range(DC):
                        sp.dma_start(u_raw[:, c], u_dram[:, P * K * c:P * K * (c + 1)].rearrange(
                            "b (p k) -> p b k", k=K)).then_inc(u_moved, 16)
                elif s[0] == "out":
                    _, b, t = s
                    done(sp, s)
                    sp.dma_start(out[b, P * t:P * (t + 1), :], x_nat[:, b, t, :]).then_inc(stored, 16)
            sp.wait_ge(stored, 16 * TT * B)

        @block.gpsimd
        def _(pool):
            nc.gpsimd.memset(ident[:], 0.0).then_inc(chain_p, 1)
            pool.wait_ge(chain_p, 1)
            nc.gpsimd.affine_select(out=ident[:], in_=ident[:], compare_op=ALU.not_equal, fill=1.0, base=0,
                                    pattern=[[-1, P]], channel_multiplier=1).then_inc(ident_ready, 1)
            nc.gpsimd.memset(v4[:], 0.0).then_inc(v_zero, 1)
            for m in range(DEPTH + 1):
                lo, hi = (0, 1) if m == 0 else (2 ** (m - 1), 2 ** m)
                c = (2.0 ** (1 - max(m, 1)) - 2.0 ** -DEPTH) / DEPTH
                nc.gpsimd.memset(level[:, :, lo:hi], c ** 0.5)
            for e in range(E):
                nc.gpsimd.memset(rank8[:, :, e:e + 1], float(E - e))
            nc.gpsimd.memset(feat[:, :, 0:1], 1.0)
            nc.gpsimd.memset(ones[:], 1.0)
            nc.gpsimd.memset(q_bd[:], 0.0)
            nc.gpsimd.memset(u_w[:], 0.0)
            nc.gpsimd.memset(ub_row[:], 0.0).then_inc(consts, 1)
            pool.wait_ge(v_zero, 1)
            pool.dma_start(bp_b[:], bp.rearrange("(a n) -> a n", a=1).broadcast_to([P, H * DEPTH])
                           ).then_inc(ld_bp, 16)
            pool.dma_start(wo[:], Wo.rearrange("(c p) n -> p c n", p=P)).then_inc(ld_wo, 16)
            for j in range(4):
                pool.dma_start(v4[KP * j:KP * j + K, :], V).then_inc(ld_v, 16)
            pool.dma_start(gate[:], gate_w).then_inc(ld_gate, 16)
            pool.dma_start(bdec[:], b_dec[0:D * K].rearrange("(c p k) -> p c k", p=P, k=K)).then_inc(ld_bdec, 16)
            pool.dma_start(bdec_row[:], b_dec[D * K:].rearrange("(a k) -> a k", a=1).broadcast_to([B, K])
                           ).then_inc(ld_bdec, 16)
            for s in ORDER:
                if s == ("start",) or s[0] == "unit":
                    for u in (0, 1) if s == ("start",) else (s[1] + 2,):
                        if u < ALL and unit(u)[1][4]:
                            pool.wait_ge(exped, u + 1)
                            tri = prob[:, u % RING, :, 0:P]
                            nc.gpsimd.affine_select(out=tri, in_=tri, compare_op=ALU.is_ge, fill=0.0, base=0,
                                                    pattern=[[0, HG], [1, P]], channel_multiplier=-1
                                                    ).then_inc(masked, 1)
                elif s[0] == "zo":
                    _, b, hf = s
                    done(pool, ("zs", b, ALL_T if b < B - 1 else SECOND if hf else FIRST))
                    for t in (2 * hf, 2 * hf + 1):
                        ins = nc.gpsimd.tensor_tensor(zo[:, t], z_nat[:, t:t + 1, :].broadcast_to([P, E, KP]),
                                                      pick[:, t, :].unsqueeze(2).broadcast_to([P, E, KP]), ALU.mult)
                    ins.then_inc(zo_ready, 1)

        @block.scalar
        def _(act):
            act.dma_start(gam_up[:, 0:D], up_gamma).then_inc(ld_gup, 16)
            act.dma_start(gam_up[:, D:2 * D], up_beta).then_inc(ld_gup, 16)
            act.dma_start(dproj[:], down_project.rearrange("(c p) n -> p c n", p=P)).then_inc(ld_dp, 16)
            act.dma_start(uproj[0:HD, :], up_project).then_inc(ld_up, 16)
            act.dma_start(uproj[HD:2 * HD, :], up_project).then_inc(ld_up, 16)
            for s in ORDER:
                if s == ("start",) or s[0] == "unit":
                    for u in (0, 1) if s == ("start",) else (s[1] + 2,):
                        if u < ALL:
                            n = unit(u)[1][3]
                            act.wait_ge(scored, u + 1)
                            if u >= RING:
                                act.wait_ge(summed, u - RING + 1)
                                if adds(u - RING + 1):
                                    act.wait_ge(added, adds(u - RING + (place(u - RING)[1] == 0)))
                            nc.scalar.activation(prob[:, u % RING, :, 0:n], s_ps[:, u % 2, :, 0:n],
                                                 ACT.Exp).then_inc(exped, 1)
                elif s[0] == "xT" and s[1] > 0:
                    full(act, s)
                    nc.scalar.copy(x_t[:, s[1], s[2], :], bank(s)[:]).then_inc(empty(s), 1)
                elif s[0] == "down":
                    full(act, s)
                    nc.scalar.activation(act_t[:], bank(s)[:, 0:T // 2], ACT.Relu).then_inc(empty(s), 1)
                elif s[0] == "VL":
                    _, b, t = s
                    full(act, s)
                    act.wait_ge(logit_ready, TT * b + t + 1)
                    nc.scalar.copy(v_sb[b % 3][:, t, :], bank(s)[:, 0:D]).then_inc(empty(s), 1)
                    if t == TT - 1:
                        if b >= 1:
                            act.wait_ge(feat_ready, b)
                        nc.scalar.activation(sign[:], logit[:].rearrange("p t (h l) -> p (t h) l", l=DEPTH),
                                             ACT.Tanh, scale=0.5).then_inc(sign_ready, 1)
                elif s[0] == "phi":
                    _, b, g = s
                    slots = feat_h[:, g, :].rearrange("p (n t) -> p n t", t=T)
                    if b == 0 and g == 0:
                        act.wait_ge(rootc_ready, 1)
                    full(act, s)
                    if b >= 1:
                        act.wait_ge(stacked[b - 1], 16 * 4 * HG)
                    nc.scalar.activation(slots[:, 0, :], bank(s)[:], ACT.Copy, scale=rootc[:]).then_inc(high_ready, 1)
                    act.wait_ge(high_ready, NG * b + g + 1)
                    nc.scalar.copy(slots[:, 1, :], slots[:, 0, :])
                    nc.scalar.copy(slots[:, 4, :], slots[:, 0, :]).then_inc(copies_ready, 1)
                elif s[0] == "wT":
                    full(act, s)
                    nc.scalar.copy(wt[:], bank(s)[:, 0:DC * (P + E)]).then_inc(empty(s), 1)
                elif s[0] == "woT":
                    full(act, s)
                    nc.scalar.copy(wo_t[:].rearrange("p c n -> p (c n)"), bank(s)[:]).then_inc(empty(s), 1)
                elif s[0] == "eT":
                    full(act, s)
                    nc.scalar.copy(ex_t[:, s[1]].rearrange("p c n -> p (c n)"), bank(s)[:]).then_inc(empty(s), 1)
                elif s[0] == "zT":
                    _, b, ts = s
                    rows = slice(KP * ts[0], KP * (ts[-1] + 1))
                    if b == 0:
                        done(act, ("ubT",))
                    full(act, s)
                    nc.scalar.activation(z_t[rows, :], bank(s)[rows, 0:P], ACT.Identity, bias=ub_col[rows, b:b + 1]
                                         ).then_inc(empty(s), 1)
                elif s[0] == "zoT":
                    full(act, s)
                    nc.scalar.copy(zo_t[:, :, CW * s[2]:CW * (s[2] + 1)], bank(s)[:].rearrange("p (e t) -> p e t", e=2)
                                   ).then_inc(empty(s), 1)

        @block.vector
        def _(dve):
            links = [0]

            def link(ins):
                links[0] += 1
                ins.then_inc(chain_v, 1)
                dve.wait_ge(chain_v, links[0])

            def normalise(m):
                b, g, half = m // BC, m % NG, m % BC // NG
                if m >= 1:
                    dve.wait_ge(ctx_ready, m)
                link(nc.vector.reciprocal(rden[:], c_ps[m % 2][:, CW:2 * CW]))
                nc.vector.tensor_tensor(ctx_t[:, b % 2, g, CW * half:CW * (half + 1)], c_ps[m % 2][:, 0:CW], rden[:],
                                        ALU.mult).then_inc(ctx_ready, 1)

            dve.wait_ge(consts, 1)
            dve.wait_ge(ident_ready, 1)
            link(nc.vector.tensor_tensor(level_d[:], level[:].rearrange("p h f -> p (h f)"), ident[:], ALU.mult))
            nc.vector.reduce_sum(rootc[:], level_d[:], AX_X).then_inc(rootc_ready, 1)
            nc.vector.memset(cond_c[:], 0.0)
            for s in ORDER:
                kind = s[0]
                if kind == "cond":
                    full(dve, s)
                    link(nc.vector.tensor_copy(cond_b[:], bank(s)[:, 0:B].unsqueeze(2).broadcast_to([P, B, P])))
                    nc.vector.tensor_copy(cond_c[:, 0:B], bank(s)[:, 0:B]).then_inc(empty(s), 1)
                elif kind == "xT" and s[1] == 0:
                    full(dve, s)
                    nc.vector.tensor_copy(x_t[:, 0, s[2], :], bank(s)[:]).then_inc(empty(s), 1)
                elif kind == "gdn":
                    g = bank(s)[:].rearrange("p (b n) -> p b n", b=B)
                    dve.wait_ge(ld_dp, 16)
                    full(dve, s)
                    for b in s[1]:
                        ins = nc.vector.tensor_tensor(w_dn[:, b], dproj[:],
                                                      g[:, b:b + 1, 0:HD].broadcast_to([P, DC, HD]), ALU.mult)
                    link(ins)
                    for b in s[1]:
                        ins = nc.vector.tensor_tensor(w_dn[:, b], w_dn[:, b],
                                                      g[:, b:b + 1, HD:2 * HD].broadcast_to([P, DC, HD]), ALU.add)
                    ins.then_inc(empty(s), 1)
                elif kind == "gup":
                    b = s[1]
                    dve.wait_ge(ld_up, 32)
                    full(dve, s)
                    link(nc.vector.tensor_tensor(w_up[:, b, :], uproj[:], bank(s)[:, 0:D], ALU.mult))
                    nc.vector.tensor_tensor(w_up[:, b, :], w_up[:, b, :], bank(s)[:, D:2 * D], ALU.add
                                            ).then_inc(empty(s), 1)
                elif kind == "up":
                    _, b, j = s
                    full(dve, s)
                    half = slice(T // 2 * j, T // 2 * (j + 1))
                    nc.vector.tensor_tensor(h_t[:, :, half], bank(s)[:].rearrange("p (c t) -> p c t", c=DC),
                                            x_t[:, b, :, half], ALU.add).then_inc(empty(s), 1)
                elif kind == "VL":
                    _, b, t = s
                    if t == 0:
                        dve.wait_ge(ld_bp, 16)
                        if b >= 1:
                            dve.wait_ge(sign_ready, b)
                    full(dve, s)
                    nc.vector.tensor_tensor(logit[:, t, :], bank(s)[:, D:D + H * DEPTH], bp_b[:], ALU.add
                                            ).then_inc(logit_ready, 1)
                elif kind == "phi":
                    _, b, g = s
                    slots = feat_h[:, g, :].rearrange("p (n t) -> p n t", t=T)
                    dve.wait_ge(high_ready, NG * b + g + 1)
                    nc.vector.scalar_tensor_tensor(out=slots[:, 2, :], in0=bank(s)[:], scalar=rootc[:],
                                                   in1=slots[:, 0, :], op0=ALU.mult, op1=ALU.subtract
                                                   ).then_inc(empty(s), 1)
                    done(dve, s)
                    nc.vector.tensor_copy(slots[:, 3, :], slots[:, 2, :]).then_inc(halves_ready, 1)
                elif kind == "Q":
                    full(dve, s)
                    for j in range(TT):
                        ins = nc.vector.tensor_copy(q_bd[KP * j:KP * j + KP, j, :], bank(s)[KP * j:KP * j + KP, 0:E])
                    ins.then_inc(empty(s), 1)
                elif kind == "U":
                    m = s[1]
                    if m == 3:
                        dve.wait_ge(ld_bdec, 32)
                        full(dve, s)
                        nc.vector.tensor_tensor(ub_row[:, :, 0:K],
                                                bank(s)[0:B, U_PIECE:U_PIECE + K].unsqueeze(1).broadcast_to([B, TT, K]),
                                                bdec_row[:].unsqueeze(1).broadcast_to([B, TT, K]), ALU.add)
                    full(dve, s)
                    nc.vector.tensor_copy(u_row[:, U_PIECE * m:U_PIECE * (m + 1)], bank(s)[:, 0:U_PIECE]
                                          ).then_inc(empty(s), 1)
                elif kind == "ubT":
                    full(dve, s)
                    nc.vector.tensor_copy(ub_col[:], bank(s)[:, 0:B]).then_inc(empty(s), 1)
                elif kind == "Uadd":
                    dve.wait_ge(u_moved, 16 * DC)
                    for c in range(DC):
                        ins = nc.vector.tensor_tensor(u_w[:, c, :, 0:K], u_raw[:, c],
                                                      bdec[:, c:c + 1, :].broadcast_to([P, B, K]), ALU.add)
                    ins.then_inc(u_ready, 1)
                elif kind == "WoU":
                    full(dve, s)
                    nc.vector.tensor_copy(wo_u[:].rearrange("p c n -> p (c n)"), bank(s)[:, 0:DC * P]
                                          ).then_inc(empty(s), 1)
                elif kind == "G":
                    full(dve, s)
                    nc.vector.tensor_tensor(gexp[:, s[1], :], bank(s)[:, 0:D], v4[:], ALU.add
                                            ).then_inc(empty(s), 1)
                elif kind == "start":
                    pass
                elif kind == "unit":
                    u = s[1]
                    m, i = place(u)
                    if not long(m) and unit(u)[1][5]:
                        dve.wait_ge(summed, u + 1)
                        normalise(m)
                    v = u + 1
                    if v < ALL and long(place(v)[0]) and place(v)[1] > 0:
                        m, i = place(v)
                        _, (_, _, _, n, diagonal, _) = unit(v)
                        dve.wait_ge(exped, v + 1)
                        if diagonal:
                            dve.wait_ge(masked, diagonals(v))
                        if i > 1:
                            dve.wait_ge(added, adds(v) - 1)
                        acc = tiles[:, m % 2, :, CW - n:CW]
                        other = prob[:, (v - 1) % RING, :, 0:n] if i == 1 else acc
                        nc.vector.tensor_tensor(acc, other, prob[:, v % RING, :, 0:n], ALU.add).then_inc(added, 1)
                elif kind == "den":
                    dve.wait_ge(closed, longs(s[1]))
                    normalise(s[1])
                elif kind == "zs":
                    _, b, ts = s
                    nt = len(ts)
                    span = slice(ts[0], ts[-1] + 1)
                    sc = bank(s)[:, P:P + nt * E].rearrange("p (t e) -> p t e", e=E)
                    full(dve, s)
                    if b >= 1:
                        dve.wait_ge(zo_ready, 2 * b)
                    nc.vector.tensor_copy(z_nat[:, span, :].rearrange("p t k -> p (t k)"), bank(s)[:, 0:KP * nt])
                    link(nc.vector.reduce_max(smax[:, span], sc, AX_X))
                    link(nc.vector.tensor_tensor(hit[:, span], sc,
                                                 smax[:, span].unsqueeze(2).broadcast_to([P, nt, E]), ALU.is_ge))
                    link(nc.vector.tensor_tensor(key[:, span], hit[:, span], rank8[:, span], ALU.mult))
                    link(nc.vector.reduce_max(kmax[:, span], key[:, span], AX_X))
                    nc.vector.tensor_tensor(pick[:, span], key[:, span],
                                            kmax[:, span].unsqueeze(2).broadcast_to([P, nt, E]),
                                            ALU.is_equal).then_inc(empty(s), 1)
                elif kind == "out":
                    _, b, t = s
                    full(dve, s)
                    nc.vector.tensor_tensor(x_nat[:, b, t, :], bank(s)[:, 0:D], x_nat[:, b, t, :], ALU.add
                                            ).then_inc(empty(s), 1)
                elif kind == "feat":
                    b = s[1]
                    dve.wait_ge(sign_ready, b + 1)
                    if b >= 1:
                        full(dve, ("phi", b - 1, NG - 1))
                    link(nc.vector.tensor_copy(feat[:, :, 1:2], sign[:, :, 0:1]))
                    for i in range(1, DEPTH):
                        n = 2 ** i
                        ins = nc.vector.tensor_tensor(feat[:, :, n:2 * n], feat[:, :, 0:n],
                                                      sign[:, :, i:i + 1].broadcast_to([P, TT * H, n]), ALU.mult)
                        if i < DEPTH - 1:
                            link(ins)
                    ins.then_inc(feat_ready, 1)

        @block.tensor
        def _(pe):
            def mm(o, w, r, start=True, stop=True):
                return nc.tensor.matmul(o, w, r, start=start, stop=stop, skip_group_check=True)

            def scores(u):
                b, (g, kt, q0, n, _, _) = unit(u)
                if u % BU == 0:
                    pe.wait_ge(stacked[b], 16 * 4 * HG)
                if u >= 2:
                    pe.wait_ge(exped, u - 1)
                else:
                    for k in (2 + 2 * u, 3 + 2 * u):
                        pe.wait_ge(emptied[k], EARLY_TURNS[k])
                for h in range(HG):
                    ins = mm(s_ps[:, u % 2, h, 0:n],
                             st[:, b % 2, g, h, P * kt:P * (kt + 1)], st[:, b % 2, g, h, T + q0:T + q0 + n])
                ins.then_inc(scored, 1)

            def context(u):
                b, (g, kt, q0, n, diagonal, last) = unit(u)
                m, _ = place(u)
                if diagonal:
                    pe.wait_ge(masked, diagonals(u))
                pe.wait_ge(exped, u + 1)
                if kt == 0:
                    if m >= 2:
                        pe.wait_ge(ctx_ready, m - 1)
                    if u % BU == 0:
                        done(pe, ("VL", b, TT - 1))
                lo = q0 % CW
                for h in range(HG):
                    ins = mm(c_ps[m % 2][DH * h:DH * (h + 1), lo:lo + n],
                             v_sb[b % 3][:, kt, DH * (HG * g + h):DH * (HG * g + h + 1)], prob[:, u % RING, h, 0:n],
                             start=(kt == 0), stop=last)
                if not long(m):
                    for h in range(HG):
                        ins = mm(c_ps[m % 2][DH * h:DH * (h + 1), CW + lo:CW + lo + n], ones[:],
                                 prob[:, u % RING, h, 0:n], start=False, stop=last)
                ins.then_inc(summed, 1)

            def denominators(m):
                pe.wait_ge(added, (LONG - 1) * longs(m))
                for h in range(HG):
                    ins = mm(c_ps[m % 2][DH * h:DH * (h + 1), CW:2 * CW], ones[:], tiles[:, m % 2, h, :], start=False)
                ins.then_inc(closed, 1)

            pe.wait_ge(ident_ready, 1)
            for s in ORDER:
                kind = s[0]
                if kind == "start":
                    pe.wait_ge(consts, 1)
                    scores(0)
                    scores(1)
                    continue
                if kind == "unit":
                    context(s[1])
                    if s[1] + 2 < ALL:
                        scores(s[1] + 2)
                    continue
                if kind == "den":
                    denominators(s[1])
                    continue
                if kind in NO_BANK:
                    continue
                _, k, turn = WORK[s]
                o = bank(s)
                if turn:
                    pe.wait_ge(emptied[k], turn)
                if kind == "cond":
                    pe.wait_ge(ld_cond, 16)
                    ins = nc.tensor.transpose(o[:, 0:B], cond_nat[:], ident[0:B, 0:B])
                elif kind == "gdn":
                    done(pe, ("cond",))
                    pe.wait_ge(ld_gdn, 32)
                    for b in s[1]:
                        ins = mm(o[:, P * b:P * (b + 1)], cond_b[:, b, :], gam_dn[:])
                elif kind == "gup":
                    if s[1] == 0:
                        pe.wait_ge(ld_gup, 32)
                    ins = mm(o[:], cond_b[:, s[1], :], gam_up[:])
                elif kind == "xT":
                    _, b, c = s
                    if c == 0:
                        pe.wait_ge(ld_x[b], 16)
                    for t in range(TT):
                        ins = nc.tensor.transpose(o[:, P * t:P * (t + 1)], x_nat[:, b, t, P * c:P * (c + 1)], ident[:])
                elif kind == "down":
                    b = s[1]
                    if b <= 1:
                        done(pe, ("gdn", (0,) if b == 0 else (1, 2, 3)))
                    for c in range(DC):
                        done(pe, ("xT", b, c))
                    for c in range(DC):
                        for j in range(2):
                            ins = mm(o[HD * j:HD * (j + 1), 0:T // 2], w_dn[:, b, c, :],
                                     x_t[:, b, c, T // 2 * j:T // 2 * (j + 1)], start=(c == 0), stop=(c == DC - 1))
                elif kind == "up":
                    _, b, j = s
                    if j == 0:
                        done(pe, ("gup", b))
                        done(pe, ("down", b))
                    for c in range(DC):
                        ins = mm(o[:, T // 2 * c:T // 2 * (c + 1)], w_up[HD * j:HD * (j + 1), b, P * c:P * (c + 1)],
                                 act_t[HD * j:HD * (j + 1), :])
                elif kind == "VL":
                    _, b, t = s
                    if t == 0:
                        if b == 0:
                            pe.wait_ge(ld_vl, 32)
                        done(pe, ("up", b, 0))
                        done(pe, ("up", b, 1))
                    for c in range(DC):
                        ins = mm(o[:, 0:D + H * DEPTH], h_t[:, c, P * t:P * (t + 1)], w_vl[:, c, :],
                                 start=(c == 0), stop=(c == DC - 1))
                elif kind == "phi":
                    _, b, g = s
                    pe.wait_ge(feat_ready, b + 1)
                    for t in range(TT):
                        ins = nc.tensor.transpose(
                            o[:, P * t:P * (t + 1)],
                            feat[:, H * t + HG * g:H * t + HG * (g + 1), :].rearrange("p h f -> p (h f)"), ident[:])
                elif kind == "wT":
                    pe.wait_ge(ld_v, 16 * 4)
                    pe.wait_ge(ld_gate, 16)
                    for c in range(DC):
                        nc.tensor.transpose(o[:, P * c:P * (c + 1)], v4[:, P * c:P * (c + 1)], ident[:])
                        ins = nc.tensor.transpose(o[:, DC * P + E * c:DC * P + E * (c + 1)],
                                                  gate[:, P * c:P * (c + 1)], ident[0:E, 0:E])
                elif kind == "woT":
                    pe.wait_ge(ld_wo, 16)
                    for d in range(DC):
                        for c in range(DC):
                            ins = nc.tensor.transpose(o[:, D * d + P * c:D * d + P * (c + 1)],
                                                      wo[:, c, P * d:P * (d + 1)], ident[:])
                elif kind == "Q":
                    done(pe, ("wT",))
                    for c in range(DC):
                        ins = mm(o[:, 0:E], wt[:, P * c:P * (c + 1)], wt[:, DC * P + E * c:DC * P + E * (c + 1)],
                                 start=(c == 0), stop=(c == DC - 1))
                elif kind == "U":
                    m = s[1]
                    if m == 0:
                        pe.wait_ge(ld_wdec, 16)
                    for j in range(4):
                        lo = U_COLS * j + U_PIECE * m
                        ins = mm(o[KP * j:KP * (j + 1), 0:U_PIECE], cond_c[:], wdec[:, lo:lo + U_PIECE])
                    if m == 3:
                        ins = mm(o[0:KP, U_PIECE:U_PIECE + K], cond_c[:], wdec[:, D * K:(D + 1) * K])
                elif kind == "ubT":
                    done(pe, ("U", 3))
                    ins = nc.tensor.transpose(o[:, 0:B], ub_row[:].rearrange("b j k -> b (j k)"), ident[0:B, 0:B])
                elif kind == "WoU":
                    pe.wait_ge(u_ready, 1)
                    done(pe, ("woT",))
                    for c in range(DC):
                        for d in range(DC):
                            ins = mm(o[:, P * c:P * (c + 1)], wo_t[:, d, P * c:P * (c + 1)],
                                     u_w[:, d].rearrange("p b k -> p (b k)"), start=(d == 0), stop=(d == DC - 1))
                elif kind == "eT":
                    e = s[1]
                    if e == 0:
                        pe.wait_ge(ld_ex, 16)
                    for hc in range(DC):
                        for fc in range(DC):
                            ins = nc.tensor.transpose(o[:, D * hc + P * fc:D * hc + P * (fc + 1)],
                                                      ex_nat[:, e, fc, P * hc:P * (hc + 1)], ident[:])
                elif kind == "G":
                    for e in range(4):
                        done(pe, ("eT", 4 * s[1] + e))
                    for hc in range(DC):
                        for j in range(4):
                            ins = mm(o[KP * j:KP * (j + 1), 0:D], wt[:, P * hc:P * hc + KP],
                                     ex_t[:, 4 * s[1] + j, hc, :], start=(hc == 0), stop=(hc == DC - 1))
                elif kind == "zT":
                    _, b, ts = s
                    if b == 0:
                        done(pe, ("ubT",))
                        done(pe, ("WoU",))
                    pe.wait_ge(ctx_ready, BC * b + (NG if ts == FIRST else BC))
                    for c in range(2 * DC):
                        for t in ts:
                            tok = slice(P * t, P * (t + 1))
                            w = u_w[:, c, b, :] if c < DC else wo_u[:, c - DC, KP * b:KP * (b + 1)]
                            r = x_t[:, b, c, tok] if c < DC else ctx_t[:, b % 2, c - DC, tok]
                            ins = mm(o[KP * t:KP * (t + 1), 0:P], w, r, start=(c == 0), stop=(c == 2 * DC - 1))
                elif kind == "zs":
                    _, b, ts = s
                    done(pe, ("zT", b, ts))
                    if b == 0:
                        done(pe, ("Q",))
                    rows = slice(KP * ts[0], KP * (ts[-1] + 1))
                    nc.tensor.transpose(o[:, 0:KP * len(ts)], z_t[rows, :], ident[rows, rows])
                    ins = mm(o[:, P:P + len(ts) * E], z_t[rows, :],
                             q_bd[rows, ts[0]:ts[-1] + 1].rearrange("p t e -> p (t e)"))
                elif kind == "zoT":
                    _, b, hf = s
                    pe.wait_ge(zo_ready, 2 * b + hf + 1)
                    for e in range(2):
                        for i in range(2):
                            ins = nc.tensor.transpose(
                                o[:, CW * e + P * i:CW * e + P * (i + 1)],
                                zo[:, 2 * hf + i, 4 * e:4 * e + 4, :].rearrange("p e k -> p (e k)"), ident[:])
                elif kind == "out":
                    _, b, t = s
                    if b == 0 and t == 0:
                        done(pe, ("G", 0))
                        done(pe, ("G", 1))
                    tok = slice(P * t, P * (t + 1))
                    for c in range(2 * DC):
                        if c == DC:
                            done(pe, ("zoT", b, t // 2))
                        w = ctx_t[:, b % 2, c, tok] if c < DC else zo_t[:, c - DC, tok]
                        r = wo[:, c, :] if c < DC else gexp[:, c - DC, :]
                        ins = mm(o[:, 0:D], w, r, start=(c == 0), stop=(c == 2 * DC - 1))
                ins.then_inc(filled, 1)


NAMES = ["x", "cond_512", "L0_cond_down_project", "L0_cond_down_gamma", "L0_cond_down_beta", "L0_cond_up_project",
         "L0_cond_up_gamma", "L0_cond_up_beta", "L0_attn_Wp", "L0_attn_bp", "L0_attn_Wv", "L0_attn_Wo",
         "L0_cond2_W_dec", "L0_cond2_b_dec", "L0_cond2_V", "L0_ffn_gate_w", "L0_ffn_expert_w"]


def kernel(**inputs):
    import numpy as np
    import concourse.bacc as bacc
    from concourse.bass_utils import run_bass_kernel_spmd as run

    nc = bacc.Bacc("TRN2", target_bir_lowering=False, num_devices=1)
    arrays, args = {}, []
    for name in NAMES:
        a = np.ascontiguousarray(inputs[name])
        arrays["in_" + name] = a
        args.append(nc.dram_tensor("in_" + name, a.shape, mybir.dt.from_np(a.dtype), kind="ExternalInput").ap())
    args.append(nc.dram_tensor("out_x", (B, T, D), F32, kind="ExternalOutput").ap())
    build(nc, *args)
    return run(nc, [arrays], core_ids=[0]).results[0]["out_x"]
```
